# Optimizing a Trainium2 kernel written in Bass

```python
import numpy as np
import jax
import jax.numpy as jnp

def _softmax(x, axis=-1):
    return jax.nn.softmax(x, axis=axis)

def _gelu(x):
    return jax.nn.gelu(x, approximate=True)

def _silu(x):
    return jax.nn.silu(x)

def _sigmoid(x):
    return jax.nn.sigmoid(x)

def _layernorm(x, axis=-1, eps=1e-05):
    m = jnp.mean(x, axis=axis, keepdims=True)
    v = jnp.var(x, axis=axis, keepdims=True)
    return (x - m) / jnp.sqrt(v + eps)

def _scatter_add(tgt, idx, src, axis=0):
    return tgt.at[idx].add(src)

def _segment_sum(src, seg, n):
    return jax.ops.segment_sum(src, seg, n)
kernel_name = 'mk_lm_tower_d1_tok_ids256_r4_e03eda'

def setup_inputs(seed: int=0):
    np.random.seed(seed)
    _w = jnp.asarray

    def _rec_inputs():
        import jax
        import jax.numpy as jnp
        _rk = jax.random.key(seed)
        x = jax.random.randint(jax.random.fold_in(_rk, 1), (4, 512), 0, 100, jnp.int32)
        mask_BSS_b0_1 = jnp.logical_not(jnp.ones((4, 512, 512), dtype=bool))
        fside_BSS_rel_dist = jax.random.uniform(jax.random.fold_in(_rk, 22), (4, 512, 512), jnp.float32, 0.0, 1)
        return (x, mask_BSS_b0_1, fside_BSS_rel_dist)
    x, mask_BSS_b0_1, fside_BSS_rel_dist = _rec_inputs()

    def _L0_tok_setup():
        import jax, jax.numpy as jnp
        import numpy as np
        NUM_ATOMS = 100
        DIM = 64
        LN_EPS = 1e-05
        key = jax.random.key(seed)
        ks = jax.random.split(key, 10)
        b, n, d = (4, 512, DIM)
        atom_ids = jax.random.randint(ks[0], (b, n), 0, NUM_ATOMS)
        adj_mat = jax.random.randint(ks[1], (b, n, n), 0, 2).astype(bool)
        rel_dist = jax.random.uniform(ks[2], (b, n, n), dtype=jnp.float32)
        s = 1.0 / np.sqrt(d)
        params = {'atom_embed': jax.random.normal(ks[3], (NUM_ATOMS, d), jnp.float32), 'neighbor_embed': jax.random.normal(ks[4], (NUM_ATOMS, d), jnp.float32), 'w_rd': jax.random.normal(ks[5], (d,), jnp.float32), 'w1': jax.random.normal(ks[6], (2 * d, d), jnp.float32) * s, 'b1': jnp.zeros((d,), jnp.float32), 'gamma': jnp.ones((d,), jnp.float32), 'beta': jnp.zeros((d,), jnp.float32), 'w2': jax.random.normal(ks[7], (d, d), jnp.float32) * s, 'b2': jnp.zeros((d,), jnp.float32)}
        return {'atom_ids': atom_ids, 'adj_mat': adj_mat, 'rel_dist': rel_dist, **params}
    _L0_tok_all = _L0_tok_setup()
    _L0_tok_in = {k: v for k, v in _L0_tok_all.items() if k in ('atom_embed', 'neighbor_embed', 'w_rd', 'w1', 'b1', 'gamma', 'beta', 'w2', 'b2')}
    del _L0_tok_all

    def _L0_attn_setup():
        import jax, jax.numpy as jnp
        import numpy as np
        PI = np.pi
        key = jax.random.key(seed)
        ks = jax.random.split(key, 24)
        B, L, D, P, H, MAXL = (1, 512, 64, 32, 4, 4096)
        Dh = D // 2
        n = lambda k, s, sc=0.02: (jax.random.normal(k, s) * sc).astype(jnp.float32)
        z = lambda s: jnp.zeros(s, jnp.float32)
        return {'x': n(ks[0], (B, L, D), 1.0), 'pos_phases': n(ks[1], (MAXL, P), PI), 'window_deltas': jnp.arange(-2, 3, dtype=jnp.float32), 'mc_w': n(ks[2], (D, D)), 'mc_b': z((D,)), 'hop_w1': n(ks[3], (D + P, D)), 'hop_b1': z((D,)), 'hop_w2': n(ks[4], (D, H * (P + 1))), 'hop_b2': z((H * (P + 1),)), 'cpe_w': n(ks[5], (D, P)), 'cpe_b': z((P,)), 've_w': n(ks[6], (D, D)), 've_b': z((D,)), 'kce_w': n(ks[7], (D, D)), 'kce_b': z((D,)), 'ksk_w1': n(ks[8], (2 * D, D)), 'ksk_b1': z((D,)), 'ksk_w2': n(ks[9], (D, P)), 'ksk_b2': z((P,)), 'sg_w1': n(ks[10], (D, Dh)), 'sg_b1': z((Dh,)), 'sg_w2': n(ks[11], (Dh, 1)), 'sg_b2': z((1,)), 'ln_g': jnp.ones((D,), jnp.float32), 'ln_b': z((D,)), 'out_w': n(ks[12], (D, D)), 'out_b': z((D,))}
    _L0_attn_all = _L0_attn_setup()
    _L0_attn_in = {k: v for k, v in _L0_attn_all.items() if k in ('pos_phases', 'window_deltas', 'mc_w', 'mc_b', 'hop_w1', 'hop_b1', 'hop_w2', 'hop_b2', 'cpe_w', 'cpe_b', 've_w', 've_b', 'kce_w', 'kce_b', 'ksk_w1', 'ksk_b1', 'ksk_w2', 'ksk_b2', 'sg_w1', 'sg_b1', 'sg_w2', 'sg_b2', 'ln_g', 'ln_b', 'out_w', 'out_b')}
    del _L0_attn_all

    def _L0_ffn_setup():
        import jax, jax.numpy as jnp
        import numpy as np
        B, S, D, E, H, K = (4, 1024, 64, 8, 128, 2)
        key = jax.random.key(seed)
        ks = jax.random.split(key, 6)
        x = jax.random.normal(ks[0], (B, S, D), jnp.float32)
        Wg = jax.random.normal(ks[1], (D, E), jnp.float32) * 0.02
        bg = jnp.zeros((E,), jnp.float32)
        W1 = jax.random.normal(ks[2], (E, D, H), jnp.float32) * 0.02
        b1 = jnp.zeros((E, H), jnp.float32)
        W2 = jax.random.normal(ks[3], (E, H, D), jnp.float32) * 0.02
        b2 = jnp.zeros((E, D), jnp.float32)
        return {'x': x, 'Wg': Wg, 'bg': bg, 'W1': W1, 'b1': b1, 'W2': W2, 'b2': b2}
    _L0_ffn_all = _L0_ffn_setup()
    _L0_ffn_in = {k: v for k, v in _L0_ffn_all.items() if k in ('Wg', 'bg', 'W1', 'b1', 'W2', 'b2')}
    del _L0_ffn_all
    return {'x': x, 'mask_BSS_b0_1': mask_BSS_b0_1, 'fside_BSS_rel_dist': fside_BSS_rel_dist, 'L0_tok_atom_embed': _L0_tok_in['atom_embed'], 'L0_tok_neighbor_embed': _L0_tok_in['neighbor_embed'], 'L0_tok_w_rd': _L0_tok_in['w_rd'], 'L0_tok_w1': _L0_tok_in['w1'], 'L0_tok_b1': _L0_tok_in['b1'], 'L0_tok_gamma': _L0_tok_in['gamma'], 'L0_tok_beta': _L0_tok_in['beta'], 'L0_tok_w2': _L0_tok_in['w2'], 'L0_tok_b2': _L0_tok_in['b2'], 'L0_attn_pos_phases': _L0_attn_in['pos_phases'], 'L0_attn_window_deltas': _L0_attn_in['window_deltas'], 'L0_attn_mc_w': _L0_attn_in['mc_w'], 'L0_attn_mc_b': _L0_attn_in['mc_b'], 'L0_attn_hop_w1': _L0_attn_in['hop_w1'], 'L0_attn_hop_b1': _L0_attn_in['hop_b1'], 'L0_attn_hop_w2': _L0_attn_in['hop_w2'], 'L0_attn_hop_b2': _L0_attn_in['hop_b2'], 'L0_attn_cpe_w': _L0_attn_in['cpe_w'], 'L0_attn_cpe_b': _L0_attn_in['cpe_b'], 'L0_attn_ve_w': _L0_attn_in['ve_w'], 'L0_attn_ve_b': _L0_attn_in['ve_b'], 'L0_attn_kce_w': _L0_attn_in['kce_w'], 'L0_attn_kce_b': _L0_attn_in['kce_b'], 'L0_attn_ksk_w1': _L0_attn_in['ksk_w1'], 'L0_attn_ksk_b1': _L0_attn_in['ksk_b1'], 'L0_attn_ksk_w2': _L0_attn_in['ksk_w2'], 'L0_attn_ksk_b2': _L0_attn_in['ksk_b2'], 'L0_attn_sg_w1': _L0_attn_in['sg_w1'], 'L0_attn_sg_b1': _L0_attn_in['sg_b1'], 'L0_attn_sg_w2': _L0_attn_in['sg_w2'], 'L0_attn_sg_b2': _L0_attn_in['sg_b2'], 'L0_attn_ln_g': _L0_attn_in['ln_g'], 'L0_attn_ln_b': _L0_attn_in['ln_b'], 'L0_attn_out_w': _L0_attn_in['out_w'], 'L0_attn_out_b': _L0_attn_in['out_b'], 'L0_ffn_Wg': _L0_ffn_in['Wg'], 'L0_ffn_bg': _L0_ffn_in['bg'], 'L0_ffn_W1': _L0_ffn_in['W1'], 'L0_ffn_b1': _L0_ffn_in['b1'], 'L0_ffn_W2': _L0_ffn_in['W2'], 'L0_ffn_b2': _L0_ffn_in['b2']}

def reference(x, mask_BSS_b0_1, fside_BSS_rel_dist, L0_tok_atom_embed, L0_tok_neighbor_embed, L0_tok_w_rd, L0_tok_w1, L0_tok_b1, L0_tok_gamma, L0_tok_beta, L0_tok_w2, L0_tok_b2, L0_attn_pos_phases, L0_attn_window_deltas, L0_attn_mc_w, L0_attn_mc_b, L0_attn_hop_w1, L0_attn_hop_b1, L0_attn_hop_w2, L0_attn_hop_b2, L0_attn_cpe_w, L0_attn_cpe_b, L0_attn_ve_w, L0_attn_ve_b, L0_attn_kce_w, L0_attn_kce_b, L0_attn_ksk_w1, L0_attn_ksk_b1, L0_attn_ksk_w2, L0_attn_ksk_b2, L0_attn_sg_w1, L0_attn_sg_b1, L0_attn_sg_w2, L0_attn_sg_b2, L0_attn_ln_g, L0_attn_ln_b, L0_attn_out_w, L0_attn_out_b, L0_ffn_Wg, L0_ffn_bg, L0_ffn_W1, L0_ffn_b1, L0_ffn_W2, L0_ffn_b2):
    import jax
    import jax.numpy as jnp

    def _L0_tok_ref(atom_ids, adj_mat, rel_dist, atom_embed, neighbor_embed, w_rd, w1, b1, gamma, beta, w2, b2):
        import jax, jax.numpy as jnp
        import numpy as np
        NUM_ATOMS = 100
        DIM = 64
        LN_EPS = 1e-05
        n = atom_ids.shape[-1]
        eye = jnp.eye(n, dtype=bool)
        mask = adj_mat & ~eye
        embeds = atom_embed[atom_ids]
        nbr_embeds = neighbor_embed[atom_ids]
        weighted = jnp.where(mask, rel_dist, jnp.zeros((), rel_dist.dtype))
        neighbor_feats = jnp.einsum('bij,bjd->bid', weighted, nbr_embeds) * w_rd
        x = jnp.concatenate([embeds, neighbor_feats], axis=-1)
        h = x @ w1 + b1
        mu = jnp.mean(h, axis=-1, keepdims=True)
        var = jnp.mean(jnp.square(h - mu), axis=-1, keepdims=True)
        h = (h - mu) * jax.lax.rsqrt(var + LN_EPS) * gamma + beta
        h = jax.nn.silu(h)
        return h @ w2 + b2

    def _L0_attn_ref(x, pos_phases, window_deltas, mc_w, mc_b, hop_w1, hop_b1, hop_w2, hop_b2, cpe_w, cpe_b, ve_w, ve_b, kce_w, kce_b, ksk_w1, ksk_b1, ksk_w2, ksk_b2, sg_w1, sg_b1, sg_w2, sg_b2, ln_g, ln_b, out_w, out_b):
        import jax, jax.numpy as jnp
        import numpy as np
        PI = np.pi
        B, L, D = x.shape
        P = cpe_w.shape[1]
        H = hop_b2.shape[0] // (P + 1)
        gelu = lambda t: jax.nn.gelu(t, approximate=False)
        sqrtP = jnp.sqrt(jnp.float32(P))
        pp = pos_phases[:L]
        pos_cos, pos_sin = (jnp.cos(pp), jnp.sin(pp))
        content = x @ mc_w + mc_b
        mem1_cos = jnp.cumsum(pos_cos[None, :, :, None] * content[:, :, None, :], axis=1)
        mem1_sin = jnp.cumsum(pos_sin[None, :, :, None] * content[:, :, None, :], axis=1)
        off_in = jnp.concatenate([x, jnp.broadcast_to(pp[None], (B, L, P))], axis=-1)
        ao = (gelu(off_in @ hop_w1 + hop_b1) @ hop_w2 + hop_b2).reshape(B, L, H, P + 1)
        center = jnp.tanh(ao[..., :P]) * PI
        width = jax.nn.sigmoid(ao[..., -1:]) * 2 + 0.1
        Wn = window_deltas.shape[0]
        deltas = window_deltas.reshape(1, 1, 1, Wn)
        weights = jnp.exp(-0.5 * deltas ** 2 / (width ** 2 + 1e-06))
        off_ph = center[:, :, :, None, :] + deltas[..., None] * 0.1
        oc, os_ = (jnp.cos(off_ph), jnp.sin(off_ph))
        pce = pos_cos.reshape(1, L, 1, 1, P)
        pse = pos_sin.reshape(1, L, 1, 1, P)
        qc = (pce * oc - pse * os_).reshape(B, L, H * Wn, P)
        qs = (pse * oc + pce * os_).reshape(B, L, H * Wn, P)
        retrieved = (jnp.einsum('blpd,blhp->blhd', mem1_cos, qc) + jnp.einsum('blpd,blhp->blhd', mem1_sin, qs)) / sqrtP
        retrieved = retrieved.reshape(B, L, H, Wn, D)
        ws = (retrieved * weights[..., None]).sum(axis=3)
        head_out = ws / (weights.sum(axis=3, keepdims=True) + 1e-06)
        mh_out = head_out.mean(axis=2)
        key_ph = jnp.tanh(x @ cpe_w + cpe_b) * PI
        key_cos, key_sin = (jnp.cos(key_ph), jnp.sin(key_ph))
        values = x @ ve_w + ve_b
        gate = jax.nn.sigmoid(gelu(x @ sg_w1 + sg_b1) @ sg_w2 + sg_b2)
        ctx = jnp.cumsum(x @ kce_w + kce_b, axis=1)
        pos = jnp.arange(1, L + 1, dtype=x.dtype).reshape(1, L, 1)
        storage_in = jnp.concatenate([x, ctx / pos], axis=-1)
        st_ph = jnp.tanh(gelu(storage_in @ ksk_w1 + ksk_b1) @ ksk_w2 + ksk_b2) * PI
        sc, ss = (jnp.cos(st_ph), jnp.sin(st_ph))
        gv = values[:, :, None, :] * gate[..., None]
        kv_cos = jnp.cumsum(sc[..., None] * gv, axis=1)
        kv_sin = jnp.cumsum(ss[..., None] * gv, axis=1)
        gate_cum = jnp.clip(jnp.cumsum(gate, axis=1), 1.0, None)
        kv_ret = (kv_cos * key_cos[..., None] + kv_sin * key_sin[..., None]).sum(axis=2)
        kv_ret = kv_ret / (jnp.sqrt(gate_cum) * sqrtP)
        combined = mh_out + kv_ret
        mu = combined.mean(-1, keepdims=True)
        var = combined.var(-1, keepdims=True)
        lnx = (combined - mu) / jnp.sqrt(var + 1e-05) * ln_g + ln_b
        return x + (lnx @ out_w + out_b)

    def _L0_ffn_ref(x, Wg, bg, W1, b1, W2, b2):
        import jax, jax.numpy as jnp
        import numpy as np
        B, S, D, E, H, K = (4, 1024, 64, 8, 128, 2)
        Bv, Sv, Dv = x.shape
        gate_scores = x @ Wg + bg
        _, idx = jax.lax.top_k(gate_scores, K)
        mask = jax.nn.one_hot(idx, E, dtype=x.dtype).sum(axis=-2)
        xf = x.reshape(-1, Dv)
        mf = mask.reshape(-1, E)
        h = jax.nn.gelu(jnp.einsum('td,edh->teh', xf, W1) + b1[None], approximate=False)
        y = jnp.einsum('teh,ehd->ted', h, W2) + b2[None]
        out = jnp.einsum('ted,te->td', y, mf)
        return out.reshape(Bv, Sv, Dv)
    h = _L0_tok_ref(x, mask_BSS_b0_1, fside_BSS_rel_dist, L0_tok_atom_embed, L0_tok_neighbor_embed, L0_tok_w_rd, L0_tok_w1, L0_tok_b1, L0_tok_gamma, L0_tok_beta, L0_tok_w2, L0_tok_b2)
    h = h + _L0_attn_ref(_layernorm(h, axis=-1), L0_attn_pos_phases, L0_attn_window_deltas, L0_attn_mc_w, L0_attn_mc_b, L0_attn_hop_w1, L0_attn_hop_b1, L0_attn_hop_w2, L0_attn_hop_b2, L0_attn_cpe_w, L0_attn_cpe_b, L0_attn_ve_w, L0_attn_ve_b, L0_attn_kce_w, L0_attn_kce_b, L0_attn_ksk_w1, L0_attn_ksk_b1, L0_attn_ksk_w2, L0_attn_ksk_b2, L0_attn_sg_w1, L0_attn_sg_b1, L0_attn_sg_w2, L0_attn_sg_b2, L0_attn_ln_g, L0_attn_ln_b, L0_attn_out_w, L0_attn_out_b)
    h = h + _L0_ffn_ref(_layernorm(h, axis=-1), L0_ffn_Wg, L0_ffn_bg, L0_ffn_W1, L0_ffn_b1, L0_ffn_W2, L0_ffn_b2)
    return h

_drawn_inputs = setup_inputs


def setup_inputs(seed=0):
    import zlib

    import numpy as np

    out = dict(_drawn_inputs(seed))
    spreads = {'L0_tok_b1': (0.0, 0.1),
     'L0_tok_gamma': (1.0, 0.2),
     'L0_tok_beta': (0.0, 0.1),
     'L0_tok_b2': (0.0, 0.1),
     'L0_attn_mc_b': (0.0, 0.315),
     'L0_attn_hop_b1': (0.0, 0.8),
     'L0_attn_hop_b2': (0.0, 0.8),
     'L0_attn_cpe_b': (0.0, 0.8),
     'L0_attn_ve_b': (0.0, 0.1),
     'L0_attn_kce_b': (0.0, 0.8),
     'L0_attn_ksk_b1': (0.0, 0.8),
     'L0_attn_ksk_b2': (0.0, 0.8),
     'L0_attn_sg_b1': (0.0, 2.0),
     'L0_attn_ln_g': (1.0, 0.6),
     'L0_attn_ln_b': (0.0, 0.543),
     'L0_attn_out_b': (0.0, 0.1),
     'L0_ffn_bg': (0.0, 0.1),
     'L0_ffn_b1': (0.0, 0.8),
     'L0_ffn_b2': (0.0, 0.1)}
    factors = {'L0_attn_window_deltas': 64.0,
     'L0_attn_hop_w1': 8.0,
     'L0_attn_hop_w2': 8.0,
     'L0_attn_cpe_w': 8.0,
     'L0_attn_kce_w': 8.0,
     'L0_attn_ksk_w1': 8.0,
     'L0_attn_ksk_w2': 8.0,
     'L0_attn_sg_w1': 8.0,
     'L0_attn_sg_w2': 8.0,
     'L0_ffn_W1': 3.58,
     'L0_ffn_W2': 2.974}
    for name, (base, spread) in spreads.items():
        noise = np.random.default_rng([zlib.crc32(name.encode()), seed]).standard_normal(out[name].shape)
        drawn = base * np.exp(spread * noise) if base else spread * noise
        out[name] = jnp.asarray(drawn.astype(out[name].dtype))
    for name, factor in factors.items():
        out[name] = (out[name] * factor).astype(out[name].dtype)
    return out
```

```python
from contextlib import ExitStack

import numpy as np

import concourse.bass as bass
from concourse import mybir

F32 = mybir.dt.float32
F32R = mybir.dt.float32r
BF16 = mybir.dt.bfloat16
U8 = mybir.dt.uint8
I8 = mybir.dt.int8
I32 = mybir.dt.int32
ALU = mybir.AluOpType
ACT = mybir.ActivationFunctionType
AX_X = mybir.AxisListType.X

P = 128
B, L, D = 4, 512, 64
NG, NH_ = 2, 2
NC = L // P
ATOMS = 100
PH, H, W = 32, 4, 5
E, HID = 8, 128
SGH = 32
EPS = 1e-5
BIG = 2.0 ** 100
PI = float(np.float32(np.pi))
TWO_PI = 6.283185
C1 = 6.28125
C2 = float(2 * np.pi - 6.28125)
ROUND = 1.5 * 2.0 ** 23
MASK_ROWS = 32

EARLY = [("atom_T1", D + 1, ATOMS), ("neigh_T", D, ATOMS), ("w1a_b1", D + 1, D), ("w1b", D, D),
         ("w_rd", D, 1), ("part_id", P, 1), ("gamma", P, 1), ("beta", P, 1), ("w2_bd", P, P),
         ("b2_rows", P, D), ("ident", P, P), ("tri", P, P)]
LATE = [("pp_T", P, L), ("pp_tok", P, L), ("deltas", P, W), ("hop1x_bd", P, P), ("hop1p", PH, P),
        ("hop_b1", P, 1), ("ksk1x_bd", P, P), ("kce_T_bd", P, P), ("ksk1c_bd", P, P),
        ("ksk1c_dup", D, P), ("kce_b", D, 1), ("ksk_b1", P, 1), ("cpe_bd", P, P), ("cpe_b", P, 1),
        ("sg1_bd", P, 2 * SGH), ("sg_b1", 2 * SGH, 1), ("sg2_bd", 2 * SGH, 2), ("sg_b2", P, 1),
        ("ksk2_bd", P, P), ("ksk_b2", P, 1), ("mcve_bd", P, 4 * D), ("mc_b", P, D), ("ve_b", P, D),
        ("hop2c", P, P), ("hop_b2c", P, 1), ("hop2w_bd", P, 2 * H), ("hop_b2w", P, H),
        ("ln_g", P, 1), ("out_bd", P, P), ("ln_b", D, P), ("out_w", D, D), ("out_b", P, D),
        ("sel_phi", 2 * PH, 2 * P), ("sel_r", 2 * PH, 2 * P), ("fold", P, 1), ("sin_scale", P, 1),
        ("sin_bias", P, 1)]
FFN = [("wg", P, E), ("bg", P, E), ("e_w1", P, E * HID), ("e_w2", P, E * D), ("e_b2", P, D),
       ("tie", P, E), ("sel_hi", P, 1), ("sel_lo", P, 1)]


def offsets(table):
    at, out = 0, {}
    for name, rows, cols in table:
        out[name] = (rows, at, at + cols)
        at += cols
    return out, at


def tower(nc, ids, dist, mask, early, late, ffn, mrows, out):
    early_at, early_n = offsets(EARLY)
    late_at, late_n = offsets(LATE)
    ffn_at, ffn_n = offsets(FFN)
    with ExitStack() as ctx:
        def sb(name, shape, dt=F32):
            return ctx.enter_context(nc.sbuf_tensor(name, shape, dt))

        def sem(name):
            return ctx.enter_context(nc.semaphore(name))

        bank = [ctx.enter_context(nc.psum_tensor(f"bank{i}", [P, 512], F32)) for i in range(8)]

        early_sb = sb("early_sb", [P, early_n])
        late_sb = sb("late_sb", [P, late_n])
        ffn_sb = sb("ffn_sb", [P, ffn_n])

        def view(tile, table):
            return {k: tile[0:r, a:b] for k, (r, a, b) in table.items()}

        K = view(early_sb, early_at) | view(late_sb, late_at) | view(ffn_sb, ffn_at)
        ones = sb("ones", [P, 512])
        ones_bf = sb("ones_bf", [1, P], BF16)
        invpos = sb("invpos", [P, L])
        w_mean = sb("w_mean", [D + 1, 2])
        w1ac = sb("w1ac", [D + 1, D])
        w1bc = sb("w1bc", [D, D])
        tables = sb("tables", [ATOMS, 2 * D])
        half_pi = sb("half_pi", [P, 1])
        wk_bd = sb("wk_bd", [P, P])
        ksk_bias = sb("ksk_bias", [P, 1])
        outw_g = sb("outw_g", [P, P])
        row_bias = sb("row_bias", [P, D])
        ang = sb("ang", [P, 2 * L + W])
        thn_all = sb("thn_all", [P, 2 * L + W])
        tha_all = sb("tha_all", [P, 2 * L + W])
        ang_n, ang_abs = thn_all, tha_all
        ang_sin = sb("ang_sin", [P, 2 * L + W])
        ang_cos = sb("ang_cos", [P, 2 * L + W])
        d_exp = sb("d_exp", [P, W])
        sg_b2h = sb("sg_b2h", [P, 1])
        w1hi = sb("w1hi", [P, E * HID], F32R)
        w1lo = sb("w1lo", [D + MASK_ROWS, E * HID], F32R)

        onehot = sb("onehot", [ATOMS, B * L])
        neigh = sb("neigh", [P, NG, NC, NH_, D])
        dist_sb = sb("dist_sb", [P, 2, NC, L])
        mask_in = sb("mask_in", [P, B, NC, L // 4], I32)
        mask_sb = mask_in[:, :, :, :].bitcast(U8)
        wm = sb("wm", [P, 2, NC, L])
        wt = sb("wt", [P, 2, NC, P])
        sq = sb("sq", [P, 512])
        hn = sb("hn", [P, NC, NH_, D])
        f_t = sb("f_t", [P, L])
        h = sb("h", [P, NG, NC, NH_, D])
        hc = sb("hc", [P, NC, NH_, D])
        x = sb("x", [P, NG, NC, NH_, D])
        st_sum = sb("st_sum", [P, 8])
        st_r = sb("st_r", [P, 8])
        rs_v = sb("rs_v", [P, 40])
        rs_a = sb("rs_a", [P, 40])
        rs_y = sb("rs_y", [P, 40])

        x_t = sb("x_t", [P, L])
        cx = sb("cx", [P, L])
        hop_g = sb("hop_g", [P, L])
        ksk_g = sb("ksk_g", [P, L])
        sg_g = sb("sg_g", [2 * SGH, L])
        kq_t = sb("kq_t", [P, L])
        st_t = sb("st_t", [P, L])
        kq_f = sb("kq_f", [P, L])
        st_f = sb("st_f", [P, L])
        st_k = sb("st_k", [P, NC, P])
        content = sb("content", [P, NC, NH_, D])
        values = sb("values", [P, NC, NH_, D])
        zg = sb("zg", [P, 40])
        tg = sb("tg", [P, 40])
        gate = sb("gate", [P, 8])
        wexp = sb("wexp", [P, 32, W])
        wtmp = sb("wtmp", [P, 32, W])
        wden = sb("wden", [P, 32])
        csum = sb("csum", [P, 2, 32])
        wscr = sb("wscr", [P, 5, 32])
        gcr = sb("gcr", [P, 8])
        phr = sb("phr", [P, NC, NH_, 2, H])
        pr = sb("pr", [2 * PH, L])
        t_c = sb("t_c", [P, 2, L])
        th = sb("th", [P, 2, L])
        thn = thn_all[:, 0:2 * L].rearrange("p (f l) -> p f l", f=2)
        tha = tha_all[:, 0:2 * L].rearrange("p (f l) -> p f l", f=2)
        q_sc = sb("q_sc", [P, 4, L])
        q_s, q_c = q_sc[:, 0:2], q_sc[:, 2:4]
        ids_i = q_sc[0:1, :, :].rearrange("p a l -> p (a l)").bitcast(I32)
        ids_bf = t_c[0:1, :, :].rearrange("p a l -> p (a l)").bitcast(BF16)
        s_m = sb("s_m", [P, 2, 2, 2, P])
        state = sb("state", [P, 2, 320])
        comb = sb("comb", [P, NC, NH_, D])
        tmp = sb("tmp", [P, NC, NH_, D])
        cc_t = x_t
        h3 = sb("h3", [P, NG, NC, NH_, D])

        xhl = sb("xhl", [P, 8, 2 * D + D // 2], F32R)
        x2 = hc
        xp1 = sb("xp1", [P, 8 * P], F32R)
        xp2 = sb("xp2", [D + MASK_ROWS, 8 * P], F32R)
        score = sb("score", [P, 8, E])
        sel = sb("sel", [P, 8, E])
        sel2 = sb("sel2", [P, 8, E])
        best = sb("best", [P, 8])
        dist_flat = dist_sb[:, :, :, :].rearrange("p a c l -> p (a c l)")
        mrow_in = dist_flat[0:D + MASK_ROWS, 0:1024]
        mrow_lo = dist_flat[0:D + MASK_ROWS, 1024:2048]
        hid = dist_flat[:, 2048:2048 + 3 * 512].rearrange("p (s l) -> p s l", s=3)

        early_in, ids_in, late_in, ffn_in = sem("early_in"), sem("ids_in"), sem("late_in"), sem("ffn_in")
        dist_in = [sem(f"dist_in{b}") for b in range(B)]
        stored = sem("stored")
        dve_step, act_step, pool_step = sem("dve_step"), sem("act_step"), sem("pool_step")
        names = """ones_set ids_cast w1_centred tables_mm tables_set ids_mm onehot_set neigh_mm neigh_set
            wm_zero diag_off dist_masked dist_free wt_mm wt_set h1_mm h1_sq h1_norm hn_mm f_set h2_mm h_set
            x_centred x_sq x_set xt_mm xt_set cx_set ang_set trig_abs trig_set fold_mm fold_set fused_set
            hop_mm hop_set sg_mm sg_set cpe_mm kq_tanh v_mm v_set ksk_mm ksk_set z_mm zg_set tg_set ksk2_mm
            st_tanh center_mm center_tanh gate_set gate_mm gate_read kq_abs st_abs w_pre w_exp at_arg at_set phr_set
            phr_mm pr_set phi_mm th_set tha_set sin_set cos_set q_set qf_sin stf_mm stk_set s_mm s_masked
            out_mm state_mm state_set comb_read comb_centred comb_sq cc_set cct_mm cct_set attn_mm h3_set hx_set
            x2_centred x2_sq xhl_set xp1_mm xp1_set xp1_act score_mm mask_set xp2_mm xp2_set w1_hi w1_lo mrow_set
            hid_mm hid_set y_mm y_set y_read score_read kq_feat st_feat v_half pr_zero cc_read""".split()
        S = {n: sem(n) for n in names}
        block = ctx.enter_context(nc.Block())

        def v8(t):
            return t.rearrange("p c f d -> p (c f) d")

        def bc(t, n):
            return t.unsqueeze(2).broadcast_to([P, t.shape[1], n])

        def rows_bc(t, n):
            return t.unsqueeze(1).broadcast_to([P, n, t.shape[1]])

        def b3(i):
            return bank[i][:, :].rearrange("p (t d) -> p t d", d=D)

        def pair(t, c):
            return t[:, c, :, :].rearrange("p f d -> p (f d)")

        @block.sync
        def _(sp):
            sp.dma_start(early_sb[:, :], early).then_inc(early_in, 16)
            sp.dma_start(ids_i[:, :], ids).then_inc(ids_in, 16)

            def load(b):
                if b >= 2:
                    sp.wait_ge(S["dist_masked"], 2 * (b - 1))
                sp.dma_start(mask_in[:, b], mask[b].rearrange("(c p) j -> p c j", p=P)).then_inc(dist_in[b], 16)
                sp.dma_start(dist_sb[:, b % 2], dist[b].rearrange("(c p) j -> p c j", p=P)).then_inc(dist_in[b], 16)

            load(0)
            load(1)
            sp.dma_start(late_sb[:, :], late).then_inc(late_in, 16)
            load(2)
            load(3)
            sp.dma_start(ffn_sb[:, :], ffn).then_inc(ffn_in, 16)
            sp.wait_ge(S["dist_masked"], 2 * B)
            sp.dma_start(mrow_in[D:D + MASK_ROWS, :], mrows).then_inc(ffn_in, 16)
            for g in range(NG):
                for f in range(NH_):
                    sp.wait_ge(S["y_set"], g + 1)
                    sp.dma_start(out[2 * g + f].rearrange("(c p) d -> p c d", p=P),
                                 h[:, g, :, f]).then_inc(stored, 16)
            sp.wait_ge(stored, 16 * B)

        @block.gpsimd
        def _(pool):
            nc.gpsimd.memset(ones[:, :], 1.0).then_inc(S["ones_set"], 1)
            nc.gpsimd.memset(ones_bf[:, :], 1.0).then_inc(S["ones_set"], 1)
            nc.gpsimd.memset(half_pi[:, :], PI / 2).then_inc(S["ones_set"], 1)
            nc.gpsimd.iota(invpos[:, :], [[1, L]], base=1, channel_multiplier=0,
                           allow_small_or_imprecise_dtypes=True).then_inc(S["ones_set"], 1)
            nc.gpsimd.memset(xhl[:, :, 2 * D + 16:2 * D + 18].bitcast(F32), 1.0).then_inc(S["ones_set"], 1)
            nc.gpsimd.memset(xhl[:, :, 2 * D + 18:].bitcast(F32), 0.0).then_inc(S["ones_set"], 1)
            nc.gpsimd.memset(pr[:, :], 0.0).then_inc(S["ones_set"], 1)
            for b in range(B):
                if b >= 2:
                    pool.wait_ge(S["wt_mm"], NC * (b - 1))
                for k in range(2):
                    nc.gpsimd.memset(wm[:, b % 2, 2 * k:2 * k + 2], 0.0).then_inc(S["wm_zero"], 1)
                pool.wait_ge(dist_in[b], 32)
                for c in range(NC):
                    diag = mask_sb[:, b, c, c * P:(c + 1) * P].bitcast(I8)
                    nc.gpsimd.affine_select(out=diag, in_=diag, compare_op=ALU.not_equal, fill=0.0, base=0,
                                            pattern=[[-1, P]], channel_multiplier=1).then_inc(S["diag_off"], 1)
            pool.wait_ge(late_in, 16)
            for g in range(NG):
                pool.wait_ge(S["fused_set"], 1)
                pool.wait_ge(S["x_set"], g + 1)
                pool.wait_ge(S["xt_mm"], g + 1)
                nc.gpsimd.tensor_tensor(v8(x[:, g]), v8(h[:, g]), v8(x[:, g]), ALU.add).then_inc(pool_step, 1)
                pool.wait_ge(pool_step, g + 1)
                nc.gpsimd.tensor_tensor(v8(x[:, g]), v8(x[:, g]), rows_bc(row_bias[:, :], 8),
                                        ALU.add).then_inc(S["hx_set"], 1)

        @block.scalar
        def _(act):
            def token(g):
                act.wait_ge(S["neigh_mm"], g + 1)
                nc.scalar.copy(v8(neigh[:, g]), b3(7 if g == 0 else 4)).then_inc(S["neigh_set"], 1)

            def distances(g):
                for k in range(8 * g, 8 * g + 8):
                    act.wait_ge(S["wt_mm"], k + 1)
                    if k >= 2:
                        act.wait_ge(S["h1_mm"], k - 1)
                    nc.scalar.copy(wt[:, k % 2].rearrange("p c i -> p (c i)"),
                                   bank[5 + k % 2][:, :]).then_inc(S["wt_set"], 1)
                act.wait_ge(S["h1_mm"], 8 * g + 8)
                if g:
                    act.wait_ge(S["x_set"], g)
                nc.scalar.activation(sq[:, :], bank[7][:, :], ACT.Square).then_inc(S["h1_sq"], 1)
                act.wait_ge(S["hn_mm"], g + 1)
                nc.scalar.activation(f_t[:, :], bank[5][:, :], ACT.Silu, bias=K["beta"],
                                     scale=K["gamma"]).then_inc(S["f_set"], 1)
                act.wait_ge(S["x_centred"], g + 1)
                nc.scalar.activation(sq[:, :], hc[:].rearrange("p c f d -> p (c f d)"),
                                     ACT.Square).then_inc(S["x_sq"], 1)

            def position_trig():
                act.wait_ge(S["ones_set"], 7)
                act.wait_ge(S["trig_abs"], 1)
                nc.scalar.activation(ang_sin[:, :], ang[:, :], ACT.Sin).then_inc(S["trig_set"], 1)
                nc.scalar.activation(ang_cos[:, :], ang_abs[:, :], ACT.Sin, bias=half_pi[:, :],
                                     scale=-1.0).then_inc(S["trig_set"], 1)

            def attention(g):
                act.wait_ge(S["xt_mm"], g + 1)
                if g:
                    act.wait_ge(S["v_mm"], 2 * g)
                    act.wait_ge(S["ksk_mm"], g)
                nc.scalar.copy(x_t[:, :], bank[0][:, :]).then_inc(S["xt_set"], 1)
                act.wait_ge(S["hop_mm"], g + 1)
                if g:
                    act.wait_ge(S["center_mm"], 2 * g)
                nc.scalar.activation(hop_g[:, :], bank[1][:, :], ACT.Gelu, bias=K["hop_b1"]).then_inc(S["hop_set"], 1)
                act.wait_ge(S["sg_mm"], g + 1)
                nc.scalar.activation(sg_g[:, :], bank[2][0:2 * SGH, :], ACT.Gelu,
                                     bias=K["sg_b1"]).then_inc(S["sg_set"], 1)
                act.wait_ge(S["cpe_mm"], g + 1)
                nc.scalar.activation(kq_t[:, :], bank[3][:, :], ACT.Tanh, bias=K["cpe_b"]).then_inc(S["kq_tanh"], 1)
                act.wait_ge(S["ksk_mm"], g + 1)
                act.wait_ge(S["fold_set"], 1)
                nc.scalar.activation(ksk_g[:, :], bank[2][:, :], ACT.Gelu,
                                     bias=ksk_bias[:, :]).then_inc(S["ksk_set"], 1)
                act.wait_ge(S["zg_set"], g + 1)
                nc.scalar.activation(tg[:, :], zg[:, :], ACT.Tanh, scale=0.5).then_inc(S["tg_set"], 1)
                act.wait_ge(S["ksk2_mm"], g + 1)
                nc.scalar.activation(st_t[:, :], bank[3][:, :], ACT.Tanh, bias=K["ksk_b2"]).then_inc(S["st_tanh"], 1)
                for f in range(NH_):
                    act.wait_ge(S["center_mm"], 2 * g + f + 1)
                    if g:
                        act.wait_ge(S["th_set"], 2 * g)
                    nc.scalar.activation(t_c[:, f], bank[4 if f == 0 else 2][:, :], ACT.Tanh,
                                         bias=K["hop_b2c"]).then_inc(S["center_tanh"], 1)
                act.wait_ge(S["w_pre"], g + 1)
                nc.scalar.activation(wexp[:], wexp[:], ACT.Exp).then_inc(S["w_exp"], 1)
                act.wait_ge(S["at_arg"], g + 1)
                nc.scalar.activation(wscr[:, 3], wscr[:, 2], ACT.Arctan).then_inc(S["at_set"], 1)
                act.wait_ge(S["kq_abs"], g + 1)
                if g:
                    act.wait_ge(S["out_mm"], NC * g)
                nc.scalar.activation(kq_f[:, :], kq_t[:, :], ACT.Sin, bias=K["sin_bias"],
                                     scale=K["sin_scale"]).then_inc(S["kq_feat"], 1)
                act.wait_ge(S["st_abs"], g + 1)
                nc.scalar.activation(st_f[:, :], st_t[:, :], ACT.Sin, bias=K["sin_bias"],
                                     scale=K["sin_scale"]).then_inc(S["st_feat"], 1)
                for f in range(NH_):
                    act.wait_ge(S["th_set"], 2 * g + f + 1)
                    nc.scalar.activation(q_s[:, f], th[:, f], ACT.Sin, scale=TWO_PI).then_inc(S["sin_set"], 1)
                    act.wait_ge(S["tha_set"], 2 * g + f + 1)
                    nc.scalar.activation(q_c[:, f], tha[:, f], ACT.Sin, bias=half_pi[:, :],
                                         scale=-TWO_PI).then_inc(S["cos_set"], 1)
                act.wait_ge(S["stf_mm"], g + 1)
                nc.scalar.copy(st_k[:].rearrange("p c f -> p (c f)"), bank[0][:, :]).then_inc(S["stk_set"], 1)
                act.wait_ge(S["comb_centred"], g + 1)
                nc.scalar.activation(sq[:, :], comb[:].rearrange("p c f d -> p (c f d)"),
                                     ACT.Square).then_inc(S["comb_sq"], 1)
                act.wait_ge(S["cct_mm"], g + 1)
                nc.scalar.copy(cc_t[:, :], bank[2][:, :]).then_inc(S["cct_set"], 1)

            def experts(g):
                act.wait_ge(S["x2_centred"], g + 1)
                nc.scalar.activation(sq[:, :], x2[:].rearrange("p c f d -> p (c f d)"),
                                     ACT.Square).then_inc(S["x2_sq"], 1)
                if g:
                    act.wait_ge(S["hid_mm"], 16 * g)
                act.wait_ge(S["xp1_mm"], 2 * g + 2)
                nc.scalar.copy(xp1[:, 512:1024], bank[6][:, :]).then_inc(S["xp1_act"], 1)
                act.wait_ge(S["xp2_mm"], 2 * g + 2)
                nc.scalar.copy(xp2[:, 512:1024], bank[6][0:D + MASK_ROWS, :]).then_inc(S["xp2_set"], 1)
                for n in range(16):
                    act.wait_ge(S["hid_mm"], 16 * g + n + 1)
                    if n >= 3 or g:
                        act.wait_ge(S["y_mm"], 16 * g + n - 2)
                    nc.scalar.activation(hid[:, (16 * g + n) % 3], bank[5 + n % 2][:, :],
                                         ACT.Gelu).then_inc(S["hid_set"], 1)

            token(0)
            token(1)
            distances(0)
            position_trig()
            attention(0)
            distances(1)
            attention(1)
            act.wait_ge(ffn_in, 32)
            nc.scalar.copy(w1hi[:, :], K["e_w1"]).then_inc(S["w1_hi"], 1)
            nc.scalar.copy(w1lo[D:D + MASK_ROWS, :], mrow_in[D:D + MASK_ROWS, :]).then_inc(S["w1_hi"], 1)
            experts(0)
            experts(1)

        @block.tensor
        def _(pe):
            ident = K["ident"]

            def tok_tables():
                pe.wait_ge(S["w1_centred"], 2)
                nc.tensor.matmul(bank[7][0:ATOMS, 0:D], K["atom_T1"], w1ac[:, :], start=True, stop=True)
                nc.tensor.matmul(bank[7][0:ATOMS, D:2 * D], K["neigh_T"], w1bc[:, :], start=True,
                                 stop=True).then_inc(S["tables_mm"], 1)
                pe.wait_ge(S["ones_set"], 2)
                pe.wait_ge(S["ids_cast"], 1)
                for n in range(4):
                    nc.tensor.matmul(bank[n][0:ATOMS, :], ones_bf[:, 0:ATOMS], ids_bf[:, n * 512:(n + 1) * 512],
                                     start=True, stop=True).then_inc(S["ids_mm"], 1)
                pe.wait_ge(S["tables_set"], 1)
                pe.wait_ge(S["onehot_set"], 4)
                for g in range(NG):
                    for t in range(8):
                        mm = nc.tensor.matmul(b3(7 if g == 0 else 4)[:, t], onehot[:, (8 * g + t) * P:(8 * g + t + 1) * P],
                                              tables[:, D:2 * D], start=True, stop=True)
                    mm.then_inc(S["neigh_mm"], 1)

            def distances(g):
                def turn(k):
                    b, c = k // NC, k % NC
                    pe.wait_ge(S["dist_masked"], 2 * b + c // 2 + 1)
                    if k >= 2:
                        pe.wait_ge(S["wt_set"], k - 1)
                    if g and k < 8 * g + 2:
                        pe.wait_ge(S["f_set"], g)
                        pe.wait_ge(S["h_set"], g)
                    for j in range(NC):
                        mm = nc.tensor.transpose(bank[5 + k % 2][:, j * P:(j + 1) * P], wm[:, b % 2, c, j * P:(j + 1) * P], ident)
                    mm.then_inc(S["wt_mm"], 1)

                def weigh(k):
                    b, c = k // NC, k % NC
                    t = c * 2 + b % 2
                    if k == 8 * g:
                        pe.wait_ge(S["neigh_set"], g + 1)
                        if g:
                            pe.wait_ge(S["h1_norm"], g)
                    at = 8 * g + t
                    nc.tensor.matmul(b3(7)[:, t], onehot[:, at * P:(at + 1) * P], tables[:, 0:D], start=True, stop=False)
                    pe.wait_ge(S["wt_set"], k + 1)
                    for j in range(NC):
                        mm = nc.tensor.matmul(b3(7)[:, t], wt[:, k % 2, j], neigh[:, g, j, b % 2],
                                              start=False, stop=(j == NC - 1))
                    mm.then_inc(S["h1_mm"], 1)

                turn(8 * g)
                for k in range(8 * g, 8 * g + 8):
                    if k + 1 < 8 * g + 8:
                        turn(k + 1)
                    weigh(k)
                pe.wait_ge(S["h1_norm"], g + 1)
                pe.wait_ge(S["wt_set"], 8 * g + 8)
                for c in range(NC):
                    mm = nc.tensor.transpose(bank[5][:, c * P:(c + 1) * P], pair(hn, c), ident)
                mm.then_inc(S["hn_mm"], 1)
                pe.wait_ge(S["f_set"], g + 1)
                for c in range(NC):
                    mm = nc.tensor.matmul(bank[6][:, c * P:(c + 1) * P], f_t[:, c * P:(c + 1) * P], K["w2_bd"],
                                          start=True, stop=True)
                mm.then_inc(S["h2_mm"], 1)

            def fold():
                pe.wait_ge(late_in, 16)
                pe.wait_ge(S["neigh_set"], 2)
                pe.wait_ge(S["onehot_set"], 4)
                nc.tensor.matmul(bank[4][:, 0:P], K["kce_T_bd"], K["ksk1c_bd"], start=True, stop=True)
                nc.tensor.matmul(bank[4][:, P:P + 1], K["ksk1c_dup"], K["kce_b"], start=True, stop=True)
                nc.tensor.matmul(bank[4][:, P + 64:P + 64 + D], K["ln_b"], K["out_w"], start=True,
                                 stop=True).then_inc(S["fold_mm"], 1)

            def attention(g):
                if g:
                    pe.wait_ge(S["comb_read"], 2 * g)
                pe.wait_ge(S["x_set"], g + 1)
                for c in range(NC):
                    mm = nc.tensor.transpose(bank[0][:, c * P:(c + 1) * P], pair(x[:, g], c), ident)
                mm.then_inc(S["xt_mm"], 1)
                pe.wait_ge(S["xt_set"], g + 1)
                if g:
                    pe.wait_ge(S["state_set"], (NC - 1) * g)
                nc.tensor.matmul(bank[1][:, :], K["hop1x_bd"], x_t[:, :], start=True, stop=False)
                nc.tensor.matmul(bank[1][:, :], K["hop1p"], K["pp_T"][0:PH, :], start=False,
                                 stop=True).then_inc(S["hop_mm"], 1)
                if g:
                    pe.wait_ge(S["cct_set"], g)
                    pe.wait_ge(S["h3_set"], g)
                nc.tensor.matmul(bank[2][0:2 * SGH, :], K["sg1_bd"], x_t[:, :], start=True,
                                 stop=True).then_inc(S["sg_mm"], 1)
                nc.tensor.matmul(bank[3][:, :], K["cpe_bd"], x_t[:, :], start=True, stop=True).then_inc(S["cpe_mm"], 1)
                pe.wait_ge(S["fold_set"], 1)
                for n, i in ((0, 4), (1, 0)):
                    for c in (0, 1):
                        mm = nc.tensor.matmul(bank[i][:, c * 256:(c + 1) * 256],
                                              x_t[:, (2 * n + c) * P:(2 * n + c + 1) * P], K["mcve_bd"],
                                              start=True, stop=True)
                    mm.then_inc(S["v_mm"], 1)
                pe.wait_ge(S["sg_set"], g + 1)
                nc.tensor.matmul(bank[2][:, :], K["ksk1x_bd"], x_t[:, :], start=True, stop=False)
                pe.wait_ge(S["cx_set"], g + 1)
                nc.tensor.matmul(bank[2][:, :], wk_bd[:, :], cx[:, :], start=False, stop=True).then_inc(S["ksk_mm"], 1)
                pe.wait_ge(S["hop_set"], g + 1)
                for c in range(NC):
                    nc.tensor.matmul(bank[1][:, c * 8:(c + 1) * 8], hop_g[:, c * P:(c + 1) * P], K["hop2w_bd"],
                                     start=True, stop=True)
                for c in range(NC):
                    mm = nc.tensor.matmul(bank[1][:, 32 + c * 2:34 + c * 2], sg_g[:, c * P:(c + 1) * P], K["sg2_bd"],
                                          start=True, stop=True)
                mm.then_inc(S["z_mm"], 1)
                pe.wait_ge(S["v_half"], 2 * g + 1)
                nc.tensor.matmul(bank[4][:, :], K["hop2c"][0:D, :], hop_g[0:D, :], start=True,
                                 stop=True).then_inc(S["center_mm"], 1)
                pe.wait_ge(S["ksk_set"], g + 1)
                nc.tensor.matmul(bank[2][:, :], K["hop2c"][D:P, :], hop_g[D:P, :], start=True,
                                 stop=True).then_inc(S["center_mm"], 1)
                pe.wait_ge(S["kq_tanh"], g + 1)
                nc.tensor.matmul(bank[3][:, :], K["ksk2_bd"], ksk_g[:, :], start=True, stop=True).then_inc(S["ksk2_mm"], 1)
                pe.wait_ge(S["gate_set"], g + 1)
                pe.wait_ge(S["zg_set"], g + 1)
                nc.tensor.matmul(bank[1][:, 0:8], K["tri"], gate[:, :], start=True, stop=True)
                for n in range(1, NC):
                    mm = nc.tensor.matmul(bank[1][:, 2 * n:8], ones[:, 0:P], gate[:, 0:8 - 2 * n], start=False,
                                          stop=True, skip_group_check=True)
                mm.then_inc(S["gate_mm"], 1)
                pe.wait_ge(S["phr_set"], g + 1)
                pe.wait_ge(S["v_half"], 2 * g + 2)
                for c in range(NC):
                    mm = nc.tensor.transpose(bank[0][0:16, c * P:(c + 1) * P],
                                             phr[:, c].rearrange("p f k h -> p (f k h)"), ident)
                mm.then_inc(S["phr_mm"], 1)
                pe.wait_ge(S["pr_set"], g + 1)
                pe.wait_ge(S["center_tanh"], 2 * g + 2)
                pe.wait_ge(S["st_tanh"], g + 1)
                pe.wait_ge(S["gate_read"], g + 1)
                for f, i, j in ((0, 4, 3), (1, 2, 1)):
                    nc.tensor.matmul(bank[i][:, :], K["sel_phi"][:, f * P:(f + 1) * P], pr[:, :], start=True, stop=True)
                    nc.tensor.matmul(bank[j][:, :], K["sel_r"][:, f * P:(f + 1) * P], pr[:, :], start=True,
                                     stop=True).then_inc(S["phi_mm"], 1)
                pe.wait_ge(S["st_feat"], g + 1)
                for c in range(NC):
                    mm = nc.tensor.transpose(bank[0][:, c * P:(c + 1) * P], st_f[:, c * P:(c + 1) * P], ident)
                mm.then_inc(S["stf_mm"], 1)
                pe.wait_ge(S["q_set"], 2 * g + 2)
                pe.wait_ge(S["kq_feat"], g + 1)
                pe.wait_ge(S["stk_set"], g + 1)

                def scores(c):
                    cols = slice(c * P, (c + 1) * P)
                    for f in range(NH_):
                        rows = slice(f * D, (f + 1) * D)
                        if c:
                            pe.wait_ge(S["s_masked"], 2 * (g * NC + c) - 1 + f)
                        nc.tensor.matmul(bank[2 + f][:, 0:P], ang_cos[:, cols], q_c[:, f, cols], start=True, stop=False)
                        nc.tensor.matmul(bank[2 + f][:, 0:P], ang_sin[:, cols], q_s[:, f, cols], start=False, stop=True)
                        nc.tensor.matmul(bank[2 + f][:, P:2 * P], st_f[rows, cols], kq_f[rows, cols], start=True,
                                         stop=True).then_inc(S["s_mm"], 1)

                def chunk_state(c):
                    if c:
                        pe.wait_ge(S["state_set"], (NC - 1) * g + c)
                    tok = slice(L + c * P, L + (c + 1) * P)
                    nc.tensor.matmul(bank[1][:, 0:P], ang_cos[:, tok], pair(content, c), start=True, stop=True)
                    nc.tensor.matmul(bank[1][:, P:2 * P], ang_sin[:, tok], pair(content, c), start=True, stop=True)
                    for f in range(NH_):
                        mm = nc.tensor.matmul(bank[1][f * D:(f + 1) * D, 2 * P:2 * P + D],
                                              st_k[:, c, f * D:(f + 1) * D], values[:, c, f], start=True, stop=True)
                    mm.then_inc(S["state_mm"], 1)

                def outputs(c):
                    cols = slice(c * P, (c + 1) * P)
                    last = state[:, (c - 1) % 2]
                    if c:
                        pe.wait_ge(S["state_set"], (NC - 1) * g + c)
                    for f, i in ((0, 4), (1, 0)):
                        rows = slice(f * D, (f + 1) * D)
                        o1, o2 = bank[i][:, c * P:c * P + D], bank[i][:, c * P + D:(c + 1) * P]
                        pe.wait_ge(S["s_masked"], 2 * (g * NC + c) + f + 1)
                        nc.tensor.matmul(o1, s_m[:, c % 2, f, 0], content[:, c, f], start=True, stop=(c == 0))
                        if c:
                            nc.tensor.matmul(o1, q_c[:, f, cols], last[:, f * D:(f + 1) * D], start=False, stop=False)
                            nc.tensor.matmul(o1, q_s[:, f, cols], last[:, P + f * D:P + (f + 1) * D], start=False, stop=True)
                        mm = nc.tensor.matmul(o2, s_m[:, c % 2, f, 1], values[:, c, f], start=True, stop=(c == 0))
                        if c:
                            mm = nc.tensor.matmul(o2, kq_f[rows, cols], last[rows, 2 * P:2 * P + D], start=False, stop=True)
                    mm.then_inc(S["out_mm"], 1)

                scores(0)
                for c in range(NC):
                    if c + 1 < NC:
                        scores(c + 1)
                        chunk_state(c)
                    outputs(c)
                pe.wait_ge(S["comb_centred"], g + 1)
                pe.wait_ge(S["s_masked"], 2 * NC * (g + 1))
                for c in range(NC):
                    mm = nc.tensor.transpose(bank[2][:, c * P:(c + 1) * P], pair(comb, c), ident)
                mm.then_inc(S["cct_mm"], 1)
                pe.wait_ge(S["cct_set"], g + 1)
                for c in range(NC):
                    mm = nc.tensor.matmul(bank[3][:, c * P:(c + 1) * P], cc_t[:, c * P:(c + 1) * P], outw_g[:, :],
                                          start=True, stop=True)
                mm.then_inc(S["attn_mm"], 1)

            def experts(g):
                if g == 0:
                    pe.wait_ge(S["h_set"], NG)
                    pe.wait_ge(S["f_set"], NG)
                else:
                    pe.wait_ge(S["hid_set"], 16 * g)
                pe.wait_ge(S["xhl_set"], g + 1)
                f32 = xhl[:].bitcast(F32)
                for n in range(2):
                    for t in range(4):
                        mm = nc.tensor.transpose(bank[5 + n][:, t * P:(t + 1) * P], f32[:, 4 * n + t, 0:2 * D], ident)
                    mm.then_inc(S["xp1_mm"], 1)
                pe.wait_ge(S["xp1_set"], g + 1)
                pe.wait_ge(S["xp1_act"], g + 1)
                pe.wait_ge(S["y_set"], g) if g else pe.wait_ge(S["h1_norm"], NG)
                for t in range(8):
                    mm = nc.tensor.matmul(bank[7][:, t * E:(t + 1) * E], xp1[:, t * P:(t + 1) * P].bitcast(F32), K["wg"],
                                          start=True, stop=True)
                mm.then_inc(S["score_mm"], 1)
                pe.wait_ge(S["mask_set"], g + 1)
                for n in range(2):
                    for t in range(4):
                        mm = nc.tensor.transpose(bank[5 + n][0:D + MASK_ROWS, t * P:(t + 1) * P],
                                                 f32[:, 4 * n + t, D:2 * D + MASK_ROWS], ident)
                    mm.then_inc(S["xp2_mm"], 1)
                pe.wait_ge(S["xp2_set"], 2 * g + 2)
                pe.wait_ge(S["w1_hi"], 2)
                pe.wait_ge(S["w1_lo"], 2)
                pe.wait_ge(S["score_read"], g + 1)
                for t in range(8):
                    nc.tensor.matmul(b3(7)[:, t], xp2[D:D + MASK_ROWS, t * P:(t + 1) * P].bitcast(F32),
                                     K["e_b2"][D:D + MASK_ROWS, :], start=(t == 0), stop=False, skip_group_check=True)

                def hidden(n):
                    e, k = n // 2, n % 2
                    if n >= 2:
                        pe.wait_ge(S["hid_set"], 16 * g + n - 1)
                    toks = slice(k * 512, (k + 1) * 512)
                    nc.tensor.matmul(bank[5 + n % 2][:, :], w1hi[:, e * HID:(e + 1) * HID], xp1[:, toks],
                                     start=True, stop=False)
                    nc.tensor.matmul(bank[5 + n % 2][:, :], w1lo[:, e * HID:(e + 1) * HID], xp2[:, toks],
                                     start=False, stop=True).then_inc(S["hid_mm"], 1)

                def back(n):
                    e, k = n // 2, n % 2
                    pe.wait_ge(S["hid_set"], 16 * g + n + 1)
                    for t in range(4):
                        mm = nc.tensor.matmul(b3(7)[:, 4 * k + t], hid[:, (16 * g + n) % 3, t * P:(t + 1) * P],
                                              K["e_w2"][:, e * D:(e + 1) * D], start=False, stop=(e == E - 1),
                                              skip_group_check=True)
                    mm.then_inc(S["y_mm"], 1)

                hidden(0)
                for n in range(16):
                    if n + 1 < 16:
                        hidden(n + 1)
                    back(n)

            tok_tables()
            distances(0)
            fold()
            attention(0)
            distances(1)
            attention(1)
            experts(0)
            experts(1)

        @block.vector
        def _(dve):
            steps = [0]

            def link(ins):
                steps[0] += 1
                ins.then_inc(dve_step, 1)
                dve.wait_ge(dve_step, steps[0])

            def magnitude(dst, src):
                return nc.vector.tensor_scalar(dst.bitcast(I32), src.bitcast(I32), 0x7FFFFFFF, None, ALU.bitwise_and)

            def rsqrt(out_ap, n):
                v, a, y = rs_v[:, 0:n], rs_a[:, 0:n], rs_y[:, 0:n]
                link(nc.vector.tensor_scalar(a.bitcast(I32), v.bitcast(I32), 1, None, ALU.logical_shift_right))
                link(nc.vector.tensor_scalar(y.bitcast(I32), a.bitcast(I32), -1.0, float(0x5F3759DF), ALU.mult, ALU.add))
                for i in range(3):
                    link(nc.vector.tensor_tensor(a, y, y, ALU.mult))
                    link(nc.vector.scalar_tensor_tensor(out=a, in0=a, scalar=-0.5, in1=v, op0=ALU.mult, op1=ALU.mult))
                    link(nc.vector.scalar_tensor_tensor(out=out_ap if i == 2 else y, in0=a, scalar=1.5, in1=y,
                                                        op0=ALU.add, op1=ALU.mult))

            def variance():
                link(nc.vector.tensor_reduce(st_sum[:, :], sq[:, :].rearrange("p (t d) -> p t d", d=D), AX_X, ALU.add))
                link(nc.vector.tensor_scalar(rs_v[:, 0:8], st_sum[:, :], 1.0 / D, EPS, ALU.mult, ALU.add))

            def centre(dst, src, done):
                link(nc.vector.tensor_reduce(st_sum[:, :], src, AX_X, ALU.add))
                link(nc.vector.tensor_scalar(st_sum[:, :], st_sum[:, :], -1.0 / D, None, ALU.mult))
                nc.vector.tensor_tensor(dst, src, bc(st_sum[:, :], D), ALU.add).then_inc(S[done], 1)

            def tok_tables():
                dve.wait_ge(early_in, 16)
                nc.vector.tensor_reduce(w_mean[:, 0:1], K["w1a_b1"], AX_X, ALU.add)
                link(nc.vector.tensor_reduce(w_mean[0:D, 1:2], K["w1b"], AX_X, ALU.add))
                link(nc.vector.tensor_scalar(w_mean[:, 0:1], w_mean[:, 0:1], -1.0 / D, None, ALU.mult))
                link(nc.vector.tensor_scalar(w_mean[0:D, 1:2], w_mean[0:D, 1:2], -1.0 / D, None, ALU.mult))
                nc.vector.tensor_scalar(w1ac[:, :], K["w1a_b1"], w_mean[:, 0:1], None, ALU.add).then_inc(S["w1_centred"], 1)
                nc.vector.tensor_scalar(w1bc[:, :], K["w1b"], w_mean[0:D, 1:2], K["w_rd"], ALU.add,
                                        ALU.mult).then_inc(S["w1_centred"], 1)
                dve.wait_ge(ids_in, 16)
                nc.vector.tensor_copy(ids_bf[:, :], ids_i[:, :]).then_inc(S["ids_cast"], 1)
                dve.wait_ge(S["tables_mm"], 1)
                nc.vector.tensor_copy(tables[:, :], bank[7][0:ATOMS, 0:2 * D]).then_inc(S["tables_set"], 1)
                for n in range(4):
                    dve.wait_ge(S["ids_mm"], n + 1)
                    nc.vector.tensor_scalar(onehot[:, n * 512:(n + 1) * 512], bank[n][0:ATOMS, :],
                                            K["part_id"][0:ATOMS, :], None, ALU.is_equal).then_inc(S["onehot_set"], 1)

            def mask_batch(b):
                dve.wait_ge(dist_in[b], 32)
                dve.wait_ge(S["diag_off"], NC * (b + 1))
                dve.wait_ge(S["wm_zero"], 2 * (b + 1))
                for k in range(2):
                    rows = slice(2 * k, 2 * k + 2)
                    nc.vector.copy_predicated(wm[:, b % 2, rows], mask_sb[:, b, rows],
                                              dist_sb[:, b % 2, rows]).then_inc(S["dist_masked"], 1)

            def token(g):
                dve.wait_ge(S["h1_sq"], g + 1)
                variance()
                rsqrt(st_r[:, :], 8)
                nc.vector.tensor_tensor(v8(hn[:]), b3(7), bc(st_r[:, :], D), ALU.mult).then_inc(S["h1_norm"], 1)
                dve.wait_ge(S["h2_mm"], g + 1)
                nc.vector.tensor_tensor(v8(h[:, g]), b3(6), rows_bc(K["b2_rows"], 8), ALU.add).then_inc(S["h_set"], 1)
                dve.wait_ge(S["h_set"], g + 1)
                centre(v8(hc[:]), v8(h[:, g]), "x_centred")
                dve.wait_ge(S["x_sq"], g + 1)
                variance()
                rsqrt(st_r[:, :], 8)
                nc.vector.tensor_tensor(v8(x[:, g]), v8(hc[:]), bc(st_r[:, :], D), ALU.mult).then_inc(S["x_set"], 1)

            def constants():
                dve.wait_ge(late_in, 16)
                dve.wait_ge(S["ones_set"], 7)
                n2 = 2 * L
                nc.vector.tensor_copy(ang[:, 0:n2], late_sb[:, late_at["pp_T"][1]:late_at["pp_tok"][2]])
                link(nc.vector.tensor_scalar(ang[:, n2:], K["deltas"], 0.1, None, ALU.mult))
                link(nc.vector.tensor_scalar(ang_n[:, :], ang[:, :], 1.0 / (2 * np.pi), ROUND, ALU.mult, ALU.add))
                link(nc.vector.tensor_scalar(ang_n[:, :], ang_n[:, :], ROUND, None, ALU.subtract))
                link(nc.vector.scalar_tensor_tensor(out=ang[:, :], in0=ang_n[:, :], scalar=-C1, in1=ang[:, :],
                                                    op0=ALU.mult, op1=ALU.add))
                link(nc.vector.scalar_tensor_tensor(out=ang[:, :], in0=ang_n[:, :], scalar=-C2, in1=ang[:, :],
                                                    op0=ALU.mult, op1=ALU.add))
                link(nc.vector.tensor_scalar(ang[:, :], ang[:, :], TWO_PI / 2, -TWO_PI / 2, ALU.min, ALU.max))
                magnitude(ang_abs[:, :], ang[:, :]).then_inc(S["trig_abs"], 1)
                nc.vector.tensor_scalar(pr[PH:2 * PH, :], ang[PH:2 * PH, 0:L], 1.0 / (2 * np.pi), None, ALU.mult)
                link(nc.vector.reciprocal(invpos[:, :], invpos[:, :]))
                nc.vector.tensor_scalar(sg_b2h[:, :], K["sg_b2"], 1.0, None, ALU.mult)
                link(nc.vector.tensor_tensor(d_exp[:, :], K["deltas"], K["deltas"], ALU.mult))
                link(nc.vector.tensor_scalar(d_exp[:, :], d_exp[:, :], -0.5, None, ALU.mult))
                nc.vector.tensor_scalar(outw_g[:, :], K["out_bd"], K["ln_g"], None, ALU.mult)
                dve.wait_ge(S["fold_mm"], 1)
                nc.vector.tensor_tensor(row_bias[:, :], bank[4][:, P + 64:P + 64 + D], K["out_b"],
                                        ALU.add).then_inc(S["fused_set"], 1)
                nc.vector.tensor_tensor(ksk_bias[:, :], bank[4][:, P:P + 1], K["ksk_b1"], ALU.add)
                nc.vector.tensor_copy(wk_bd[:, :], bank[4][:, 0:P]).then_inc(S["fold_set"], 1)

            def attention(g):
                dve.wait_ge(S["xt_set"], g + 1)
                if g:
                    dve.wait_ge(S["ksk_mm"], g)
                link(nc.vector.tensor_tensor_scan(cx[:, :], ones[:, :], x_t[:, :], 0.0, ALU.mult, ALU.add))
                nc.vector.tensor_tensor(cx[:, :], cx[:, :], invpos[:, :], ALU.mult).then_inc(S["cx_set"], 1)
                for n, i in ((0, 4), (1, 0)):
                    dve.wait_ge(S["v_mm"], 2 * g + n + 1)
                    src = bank[i][:, :].rearrange("p (c k f d) -> p c k f d", c=2, k=2, d=D)
                    for c in range(2):
                        if g:
                            dve.wait_ge(S["out_mm"], NC * g)
                        nc.vector.tensor_tensor(content[:, 2 * n + c], src[:, c, 0], rows_bc(K["mc_b"], 2), ALU.add)
                        ins = nc.vector.tensor_tensor(values[:, 2 * n + c], src[:, c, 1], rows_bc(K["ve_b"], 2), ALU.add)
                    ins.then_inc(S["v_half"], 1)
                dve.wait_ge(S["z_mm"], g + 1)
                nc.vector.tensor_tensor(zg[:, 0:32].rearrange("p (t h) -> p t h", h=H),
                                        bank[1][:, 0:32].rearrange("p (t h) -> p t h", h=H), rows_bc(K["hop_b2w"], 8), ALU.add)
                nc.vector.tensor_scalar(zg[:, 32:40], bank[1][:, 32:40], sg_b2h[:, :], None, ALU.add).then_inc(S["zg_set"], 1)
                dve.wait_ge(S["tg_set"], g + 1)
                nc.vector.tensor_scalar(gate[:, :], tg[:, 32:40], 0.5, 0.5, ALU.mult, ALU.add).then_inc(S["gate_set"], 1)
                link(nc.vector.tensor_scalar(wden[:, :], tg[:, 0:32], 1.1, None, ALU.add))
                link(nc.vector.tensor_tensor(wden[:, :], wden[:, :], wden[:, :], ALU.mult))
                link(nc.vector.tensor_scalar(wden[:, :], wden[:, :], 1e-6, None, ALU.add))
                link(nc.vector.reciprocal(wden[:, :], wden[:, :]))
                nc.vector.tensor_tensor(wexp[:], wden[:, :].unsqueeze(2).broadcast_to([P, 32, W]),
                                        rows_bc(d_exp[:, :], 32), ALU.mult).then_inc(S["w_pre"], 1)
                dve.wait_ge(S["gate_set"], g + 1)
                link(nc.vector.tensor_tensor(v8(values[:]), v8(values[:]), bc(gate[:, :], D), ALU.mult))
                dve.wait_ge(S["kq_tanh"], g + 1)
                nc.vector.scalar_tensor_tensor(out=kq_t[:, :], in0=kq_t[:, :], scalar=K["fold"], in1=kq_t[:, :],
                                               op0=ALU.mult, op1=ALU.max).then_inc(S["kq_abs"], 1)
                dve.wait_ge(S["st_tanh"], g + 1)
                nc.vector.scalar_tensor_tensor(out=st_t[:, :], in0=st_t[:, :], scalar=K["fold"], in1=st_t[:, :],
                                               op0=ALU.mult, op1=ALU.max).then_inc(S["st_abs"], 1)
                dve.wait_ge(S["w_exp"], g + 1)
                nc.vector.tensor_reduce(wden[:, :], wexp[:], AX_X, ALU.add)
                link(nc.vector.tensor_tensor(wtmp[:], wexp[:], rows_bc(ang_cos[:, 2 * L:], 32), ALU.mult))
                nc.vector.tensor_reduce(csum[:, 0], wtmp[:], AX_X, ALU.add)
                link(nc.vector.tensor_tensor(wexp[:], wexp[:], rows_bc(ang_sin[:, 2 * L:], 32), ALU.mult))
                link(nc.vector.tensor_reduce(csum[:, 1], wexp[:], AX_X, ALU.add))
                link(nc.vector.tensor_tensor(wscr[:, 0:2], csum[:], csum[:], ALU.mult))
                link(nc.vector.tensor_tensor(wscr[:, 0], wscr[:, 0], wscr[:, 1], ALU.add))
                nc.vector.tensor_scalar(rs_v[:, 0:32], wscr[:, 0], 1e-30, None, ALU.max)
                dve.wait_ge(S["gate_mm"], g + 1)
                nc.vector.tensor_scalar(rs_v[:, 32:40], bank[1][:, 0:8], 1.0, float(PH), ALU.max,
                                        ALU.mult).then_inc(S["gate_read"], 1)
                dve.wait_ge(S["gate_read"], g + 1)
                rsqrt(rs_a[:, 0:40], 40)
                nc.vector.tensor_copy(gcr[:, :], rs_a[:, 32:40])
                link(nc.vector.tensor_tensor(wscr[:, 0], wscr[:, 0], rs_a[:, 0:32], ALU.mult))
                link(magnitude(wscr[:, 1], csum[:, 0]))
                link(nc.vector.scalar_tensor_tensor(out=wscr[:, 1], in0=wscr[:, 1], scalar=1e-30, in1=wscr[:, 0],
                                                    op0=ALU.add, op1=ALU.add))
                link(nc.vector.reciprocal(wscr[:, 1], wscr[:, 1]))
                nc.vector.tensor_tensor(wscr[:, 2], csum[:, 1], wscr[:, 1], ALU.mult).then_inc(S["at_arg"], 1)
                link(nc.vector.tensor_scalar(wden[:, :], wden[:, :], 1e-6, float(H * np.sqrt(PH)), ALU.add, ALU.mult))
                link(nc.vector.reciprocal(wden[:, :], wden[:, :]))
                r4 = phr[:].rearrange("p c f k h -> p (c f) k h")
                w4 = lambda t: t.rearrange("p (t h) -> p t h", h=H)
                nc.vector.tensor_tensor(r4[:, :, 1], w4(wscr[:, 0]), w4(wden[:, :]), ALU.mult)
                link(nc.vector.tensor_scalar(wscr[:, 4], csum[:, 0], 0.0, None, ALU.is_lt))
                dve.wait_ge(S["at_set"], g + 1)
                link(nc.vector.tensor_scalar(wscr[:, 1], wscr[:, 3], -2.0 / np.pi, 0.5, ALU.mult, ALU.add))
                link(nc.vector.tensor_tensor(wscr[:, 1], wscr[:, 1], wscr[:, 4], ALU.mult))
                nc.vector.scalar_tensor_tensor(out=r4[:, :, 0], in0=w4(wscr[:, 3]), scalar=1.0 / np.pi,
                                               in1=w4(wscr[:, 1]), op0=ALU.mult, op1=ALU.add).then_inc(S["phr_set"], 1)
                dve.wait_ge(S["phr_mm"], g + 1)
                nc.vector.tensor_copy(pr[0:16, :], bank[0][0:16, :]).then_inc(S["pr_set"], 1)
                banks = ((4, 3), (2, 1))
                for f in range(NH_):
                    dve.wait_ge(S["phi_mm"], 2 * g + f + 1)
                    dve.wait_ge(S["center_tanh"], 2 * g + f + 1)
                    link(nc.vector.scalar_tensor_tensor(out=th[:, f], in0=t_c[:, f], scalar=0.5, in1=bank[banks[f][0]][:, :],
                                                        op0=ALU.mult, op1=ALU.add))
                    link(nc.vector.tensor_scalar(thn[:, f], th[:, f], ROUND, ROUND, ALU.add, ALU.subtract))
                    nc.vector.tensor_tensor(th[:, f], th[:, f], thn[:, f], ALU.subtract).then_inc(S["th_set"], 1)
                    dve.wait_ge(S["th_set"], 2 * g + f + 1)
                    magnitude(tha[:, f], th[:, f]).then_inc(S["tha_set"], 1)
                for f in range(NH_):
                    dve.wait_ge(S["sin_set"], 2 * g + f + 1)
                    nc.vector.tensor_tensor(q_s[:, f], q_s[:, f], bank[banks[f][1]][:, :], ALU.mult)
                    dve.wait_ge(S["cos_set"], 2 * g + f + 1)
                    nc.vector.tensor_tensor(q_c[:, f], q_c[:, f], bank[banks[f][1]][:, :], ALU.mult).then_inc(S["q_set"], 1)
                tri2 = K["tri"].unsqueeze(1).broadcast_to([P, 2, P])
                for c in range(NC):
                    at = g * NC + c
                    for f in range(NH_):
                        dve.wait_ge(S["s_mm"], 2 * at + f + 1)
                        if at >= 2:
                            dve.wait_ge(S["out_mm"], at - 1)
                        nc.vector.tensor_tensor(s_m[:, c % 2, f], bank[2 + f][:, 0:2 * P].rearrange("p (k l) -> p k l", k=2),
                                                tri2, ALU.mult).then_inc(S["s_masked"], 1)
                    if c:
                        dve.wait_ge(S["state_mm"], (NC - 1) * g + c)
                        if c == 1:
                            if g:
                                dve.wait_ge(S["out_mm"], NC * g)
                            nc.vector.tensor_copy(state[:, 0], bank[1][:, 0:320]).then_inc(S["state_set"], 1)
                        else:
                            dve.wait_ge(S["state_set"], (NC - 1) * g + c - 1)
                            if c == 3:
                                dve.wait_ge(S["out_mm"], NC * g + 2)
                            nc.vector.tensor_tensor(state[:, (c - 1) % 2], bank[1][:, 0:320], state[:, c % 2],
                                                    ALU.add).then_inc(S["state_set"], 1)
                dve.wait_ge(S["out_mm"], NC * (g + 1))
                r4g = gcr[:, :].rearrange("p (c f) -> p c f", f=2)
                for f, i in ((0, 4), (1, 0)):
                    o = bank[i][:, :].rearrange("p (c k d) -> p c k d", c=NC, k=2)
                    link(nc.vector.tensor_tensor(tmp[:, :, f], o[:, :, 1], bc(r4g[:, :, f], D), ALU.mult))
                    nc.vector.tensor_tensor(comb[:, :, f], o[:, :, 0], tmp[:, :, f], ALU.add).then_inc(S["comb_read"], 1)
                dve.wait_ge(S["comb_read"], 2 * (g + 1))
                centre(v8(comb[:]), v8(comb[:]), "comb_centred")
                dve.wait_ge(S["comb_sq"], g + 1)
                variance()
                rsqrt(st_r[:, :], 8)
                dve.wait_ge(S["attn_mm"], g + 1)
                link(nc.vector.tensor_tensor(v8(tmp[:]), b3(3), bc(st_r[:, :], D), ALU.mult))
                dve.wait_ge(S["hx_set"], g + 1)
                nc.vector.tensor_tensor(v8(h3[:, g]), v8(tmp[:]), v8(x[:, g]), ALU.add).then_inc(S["h3_set"], 1)

            def expert_weights():
                dve.wait_ge(ffn_in, 32)
                dve.wait_ge(S["w1_hi"], 2)
                hi = w1hi[:].bitcast(F32)
                nc.vector.tensor_tensor(w1lo[0:D, :], K["e_w1"][0:D, :], hi[0:D, :], ALU.subtract).then_inc(S["w1_lo"], 1)
                mr = slice(D, D + MASK_ROWS)
                link(nc.vector.tensor_tensor(mrow_lo[mr, :], mrow_in[mr, :], w1lo[mr, :].bitcast(F32), ALU.subtract))
                link(nc.vector.tensor_scalar(mrow_lo[mr, :], mrow_lo[mr, :], K["sel_lo"][mr, :], None, ALU.mult))
                nc.vector.scalar_tensor_tensor(out=w1lo[mr, :], in0=w1lo[mr, :].bitcast(F32), scalar=K["sel_hi"][mr, :],
                                               in1=mrow_lo[mr, :], op0=ALU.mult, op1=ALU.add).then_inc(S["w1_lo"], 1)

            def experts(g):
                dve.wait_ge(S["h3_set"], g + 1)
                centre(v8(x2[:]), v8(h3[:, g]), "x2_centred")
                dve.wait_ge(S["x2_sq"], g + 1)
                variance()
                rsqrt(st_r[:, :], 8)
                link(nc.vector.tensor_tensor(v8(x2[:]), v8(x2[:]), bc(st_r[:, :], D), ALU.mult))
                if g:
                    dve.wait_ge(S["xp2_mm"], 2 * g)
                link(nc.vector.tensor_copy(xhl[:, :, D:2 * D], v8(x2[:])))
                nc.vector.tensor_tensor(xhl[:, :, 0:D], v8(x2[:]), xhl[:, :, D:2 * D].bitcast(F32),
                                        ALU.subtract).then_inc(S["xhl_set"], 1)
                dve.wait_ge(S["xp1_mm"], 2 * g + 1)
                if g:
                    dve.wait_ge(S["hid_mm"], 16 * g)
                nc.vector.tensor_copy(xp1[:, 0:512], bank[5][:, :]).then_inc(S["xp1_set"], 1)
                dve.wait_ge(S["score_mm"], g + 1)
                nc.vector.tensor_tensor(score[:], bank[7][:, 0:64].rearrange("p (t e) -> p t e", e=E),
                                        rows_bc(K["bg"], 8), ALU.add).then_inc(S["score_read"], 1)
                dve.wait_ge(S["score_read"], g + 1)
                chosen = [sel, sel2]
                for k in range(2):
                    link(nc.vector.tensor_reduce(best[:, :], score[:], AX_X, ALU.max))
                    link(nc.vector.tensor_tensor(chosen[k][:], score[:], bc(best[:, :], E), ALU.is_equal))
                    link(nc.vector.tensor_tensor(chosen[k][:], chosen[k][:], rows_bc(K["tie"], 8), ALU.mult))
                    link(nc.vector.tensor_reduce(best[:, :], chosen[k][:], AX_X, ALU.max))
                    link(nc.vector.tensor_tensor(chosen[k][:], rows_bc(K["tie"], 8), bc(best[:, :], E), ALU.is_equal))
                    if k == 0:
                        link(nc.vector.scalar_tensor_tensor(out=score[:], in0=sel[:], scalar=-3.0e38, in1=score[:],
                                                            op0=ALU.mult, op1=ALU.add))
                link(nc.vector.tensor_tensor(xhl[:, :, 2 * D + E:2 * D + 2 * E], sel[:], sel2[:], ALU.add))
                nc.vector.tensor_scalar(xhl[:, :, 2 * D:2 * D + E], xhl[:, :, 2 * D + E:2 * D + 2 * E].bitcast(F32), -1.0,
                                        1.0, ALU.mult, ALU.add).then_inc(S["mask_set"], 1)
                dve.wait_ge(S["xp2_mm"], 2 * g + 1)
                nc.vector.tensor_copy(xp2[:, 0:512], bank[5][0:D + MASK_ROWS, :]).then_inc(S["xp2_set"], 1)

            def output(g):
                dve.wait_ge(S["y_mm"], 16 * (g + 1))
                nc.vector.tensor_tensor(v8(h[:, g]), b3(7), v8(h3[:, g]), ALU.add).then_inc(S["y_set"], 1)

            tok_tables()
            mask_batch(0)
            mask_batch(1)
            token(0)
            constants()
            attention(0)
            mask_batch(2)
            mask_batch(3)
            token(1)
            attention(1)
            expert_weights()
            experts(0)
            output(0)
            experts(1)
            output(1)


def kernel(x, mask_BSS_b0_1, fside_BSS_rel_dist, L0_tok_atom_embed, L0_tok_neighbor_embed, L0_tok_w_rd, L0_tok_w1,
           L0_tok_b1, L0_tok_gamma, L0_tok_beta, L0_tok_w2, L0_tok_b2, L0_attn_pos_phases, L0_attn_window_deltas,
           L0_attn_mc_w, L0_attn_mc_b, L0_attn_hop_w1, L0_attn_hop_b1, L0_attn_hop_w2, L0_attn_hop_b2, L0_attn_cpe_w,
           L0_attn_cpe_b, L0_attn_ve_w, L0_attn_ve_b, L0_attn_kce_w, L0_attn_kce_b, L0_attn_ksk_w1, L0_attn_ksk_b1,
           L0_attn_ksk_w2, L0_attn_ksk_b2, L0_attn_sg_w1, L0_attn_sg_b1, L0_attn_sg_w2, L0_attn_sg_b2, L0_attn_ln_g,
           L0_attn_ln_b, L0_attn_out_w, L0_attn_out_b, L0_ffn_Wg, L0_ffn_bg, L0_ffn_W1, L0_ffn_b1, L0_ffn_W2, L0_ffn_b2):
    import concourse.bacc as bacc
    from concourse.bass_utils import run_bass_kernel_spmd

    f = np.float32
    arr = lambda t: np.asarray(t)
    row = lambda t: np.tile(arr(t)[None, :], (P, 1))
    col = lambda t, n=1: np.tile(arr(t).reshape(-1), n)[:, None]

    def bd(w):
        w = arr(w)
        o = np.zeros((2 * w.shape[0], 2 * w.shape[1]), f)
        o[:w.shape[0], :w.shape[1]] = w
        o[w.shape[0]:, w.shape[1]:] = w
        return o

    def pack(table, parts):
        at, n = offsets(table)
        o = np.zeros((P, n), f)
        for name, (rows, a, b) in at.items():
            o[:rows, a:b] = parts[name]
        return o

    w1, ksk1, hop1 = arr(L0_tok_w1), arr(L0_attn_ksk_w1), arr(L0_attn_hop_w1)
    hop2 = arr(L0_attn_hop_w2).reshape(D, H, PH + 1)
    hopb2 = arr(L0_attn_hop_b2).reshape(H, PH + 1)
    pp = arr(L0_attn_pos_phases)[:L]
    pp_rep = np.tile(pp, (1, H))
    twice = lambda w: np.concatenate([arr(w), arr(w)], axis=1)
    early = pack(EARLY, {
        "atom_T1": np.concatenate([arr(L0_tok_atom_embed).T, np.ones((1, ATOMS), f)]),
        "neigh_T": arr(L0_tok_neighbor_embed).T,
        "w1a_b1": np.concatenate([w1[:D], arr(L0_tok_b1)[None, :]]), "w1b": w1[D:], "w_rd": col(L0_tok_w_rd),
        "part_id": np.arange(P, dtype=f)[:, None], "gamma": col(L0_tok_gamma, 2), "beta": col(L0_tok_beta, 2),
        "w2_bd": bd(L0_tok_w2), "b2_rows": row(L0_tok_b2), "ident": np.eye(P, dtype=f),
        "tri": np.triu(np.ones((P, P), f))})
    sel_phi, sel_r = np.zeros((2 * PH, 2, P), f), np.zeros((2 * PH, 2, P), f)
    for k in range(2):
        for hh in range(H):
            sel_phi[8 * k + hh, k, hh * PH:(hh + 1) * PH] = 1
            sel_r[8 * k + H + hh, k, hh * PH:(hh + 1) * PH] = 1
        for q in range(PH):
            sel_phi[PH + q, k, q::PH] = 1
    cos_row = (np.arange(P) // PH % 2 == 0)
    late = pack(LATE, {
        "pp_T": pp_rep.T, "pp_tok": pp_rep.reshape(NC, P, P).transpose(1, 0, 2).reshape(P, L),
        "deltas": row(L0_attn_window_deltas), "hop1x_bd": bd(hop1[:D]), "hop1p": twice(hop1[D:]),
        "hop_b1": col(L0_attn_hop_b1, 2), "ksk1x_bd": bd(ksk1[:D]), "kce_T_bd": bd(arr(L0_attn_kce_w).T),
        "ksk1c_bd": bd(ksk1[D:]), "ksk1c_dup": twice(ksk1[D:]), "kce_b": col(L0_attn_kce_b),
        "ksk_b1": col(L0_attn_ksk_b1, 2), "cpe_bd": bd(twice(L0_attn_cpe_w)), "cpe_b": col(L0_attn_cpe_b, 4),
        "sg1_bd": bd(L0_attn_sg_w1), "sg_b1": col(L0_attn_sg_b1, 2), "sg2_bd": bd(L0_attn_sg_w2),
        "sg_b2": col(L0_attn_sg_b2, P), "ksk2_bd": bd(twice(L0_attn_ksk_w2)), "ksk_b2": col(L0_attn_ksk_b2, 4),
        "mcve_bd": np.concatenate([bd(L0_attn_mc_w), bd(L0_attn_ve_w)], axis=1), "mc_b": row(L0_attn_mc_b),
        "ve_b": row(L0_attn_ve_b), "hop2c": np.tile(hop2[:, :, :PH].reshape(D, P), (2, 1)),
        "hop_b2c": hopb2[:, :PH].reshape(P, 1), "hop2w_bd": bd(hop2[:, :, PH]), "hop_b2w": row(hopb2[:, PH]),
        "ln_g": col(L0_attn_ln_g, 2), "out_bd": bd(L0_attn_out_w), "ln_b": np.tile(col(L0_attn_ln_b), (1, P)),
        "out_w": arr(L0_attn_out_w), "out_b": row(L0_attn_out_b), "sel_phi": sel_phi.reshape(2 * PH, 2 * P),
        "sel_r": sel_r.reshape(2 * PH, 2 * P), "fold": np.where(cos_row, -1, 1).astype(f)[:, None],
        "sin_scale": np.where(cos_row, -TWO_PI / 2, TWO_PI / 2).astype(f)[:, None],
        "sin_bias": np.where(cos_row, PI / 2, 0).astype(f)[:, None]})
    e_w1 = arr(L0_ffn_W1).transpose(1, 0, 2).reshape(D, E * HID)
    e_b2 = np.zeros((P, D), f)
    e_b2[D + E:D + 2 * E] = arr(L0_ffn_b2)
    which = np.arange(P)[:, None]
    ffn = pack(FFN, {
        "wg": np.tile(arr(L0_ffn_Wg), (2, 1)), "bg": row(L0_ffn_bg), "e_w1": np.tile(e_w1, (2, 1)),
        "e_w2": arr(L0_ffn_W2).transpose(1, 0, 2).reshape(HID, E * D), "e_b2": e_b2,
        "tie": np.tile(np.arange(E, 0, -1, dtype=f)[None, :], (P, 1)),
        "sel_hi": (which != D + 2 * E + 1).astype(f), "sel_lo": (which == D + 2 * E + 1).astype(f)})
    mrows = np.zeros((MASK_ROWS, E, HID), f)
    mrows[np.arange(E), np.arange(E)] = -BIG
    mrows[2 * E:2 * E + 2] = arr(L0_ffn_b1)
    ids = np.ascontiguousarray(arr(x).reshape(NG, NH_, NC, P).transpose(0, 2, 1, 3)).reshape(1, B * L)
    arrays = {"ids": ids, "dist": np.ascontiguousarray(arr(fside_BSS_rel_dist)),
              "mask": np.ascontiguousarray(arr(mask_BSS_b0_1)).view(np.int32),
              "early": early, "late": late, "ffn": ffn, "mrows": mrows.reshape(MASK_ROWS, E * HID)}
    nc = bacc.Bacc("TRN2", target_bir_lowering=False, num_devices=1)
    args = [nc.dram_tensor(f"in_{k}", a.shape, mybir.dt.from_np(a.dtype), kind="ExternalInput").ap()
            for k, a in arrays.items()]
    out = nc.dram_tensor("out", (B, L, D), F32, kind="ExternalOutput").ap()
    tower(nc, *args, out)
    r = run_bass_kernel_spmd(nc, [{f"in_{k}": a for k, a in arrays.items()}], core_ids=[0])
    return r.results[0]["out"]
```

```python
from contextlib import ExitStack

import numpy as np

import concourse.bass as bass
from concourse import mybir

F32 = mybir.dt.float32
F32R = mybir.dt.float32r
BF16 = mybir.dt.bfloat16
U8 = mybir.dt.uint8
I8 = mybir.dt.int8
I32 = mybir.dt.int32
ALU = mybir.AluOpType
ACT = mybir.ActivationFunctionType
AX_X = mybir.AxisListType.X

P = 128
B, L, D = 4, 512, 64
NG, NH_ = 2, 2
NC = L // P
ATOMS = 100
PH, H, W = 32, 4, 5
E, HID = 8, 128
SGH = 32
EPS = 1e-5
BIG = 2.0 ** 100
PI = float(np.float32(np.pi))
TWO_PI = 6.283185
C1 = 6.28125
C2 = float(2 * np.pi - 6.28125)
ROUND = 1.5 * 2.0 ** 23
MASK_ROWS = 32
VK = 2 * (2 * D + PH)

EARLY = [("atom_T1", D + 1, ATOMS), ("neigh_T", D, ATOMS), ("w1a_b1", D + 1, D), ("w1b", D, D),
         ("w_rd", D, 1), ("part_id", P, 1), ("gamma", P, 1), ("beta", P, 1), ("w2_bd", P, P),
         ("b2_rows", P, D), ("ident", P, P), ("tri", P, P)]
LATE = [("pp_T", PH, L), ("pp_tok", P, NC * PH), ("deltas", P, W), ("hop1x_bd", P, P), ("hop1p", PH, P),
        ("hop_b1", P, 1), ("ksk1x_bd", P, P), ("kce_T_bd", P, P), ("ksk1c_bd", P, P),
        ("ksk1c_dup", D, P), ("kce_b", D, 1), ("ksk_b1", P, 1), ("vk_bd", P, VK), ("vk_b", P, VK),
        ("sg1_bd", P, 2 * SGH), ("sg_b1", 2 * SGH, 1), ("sg2_bd", 2 * SGH, 2), ("sg_b2", P, 1),
        ("ksk2_bd", P, 2 * PH), ("ksk_b2", P, PH), ("hop2c_bd", P, 2 * P), ("hop_b2c", P, P),
        ("hop2w_bd", P, 2 * H), ("hop_b2w", P, H),
        ("ln_g", P, 1), ("out_bd", P, P), ("ln_b", D, P), ("out_w", D, D), ("out_b", P, D)]
FFN = [("wg", P, E), ("bg", P, E), ("e_w1", P, E * HID), ("e_w2", P, E * D), ("e_b2", P, D),
       ("tie", P, E), ("sel_hi", P, 1), ("sel_lo", P, 1)]

ORDER = ("T0 " * 6 + "P0 T1 P0 T1 T1 P0 T1 P0 T1 Q0 T1 Q0 P1 P1 Q0 P1 Q0 P1 C0 C0 Q1 C0 C0 Q1 C0 Q1 C0 C0 Q1 C0 "
         + "X0 C1 C1 X0 C1 X0 C1 X0 C1 X0 C1 X0 C1 C1 " + "X0 " * 7 + "X1 X0 X0 X0 X0 X0 X0 X0 " + "X1 " * 19).split()


def follow(stages):
    running = {}
    for name in ORDER:
        if name not in running:
            running[name] = stages[name[0]](int(name[1]))
        next(running[name])


def offsets(table):
    at, out = 0, {}
    for name, rows, cols in table:
        out[name] = (rows, at, at + cols)
        at += cols
    return out, at


def tower(nc, ids, dist, mask, early, late, ffn, mrows, out):
    early_at, early_n = offsets(EARLY)
    late_at, late_n = offsets(LATE)
    ffn_at, ffn_n = offsets(FFN)
    with ExitStack() as ctx:
        def sb(name, shape, dt=F32):
            return ctx.enter_context(nc.sbuf_tensor(name, shape, dt))

        def sem(name):
            return ctx.enter_context(nc.semaphore(name))

        bank = [ctx.enter_context(nc.psum_tensor(f"bank{i}", [P, 512], F32)) for i in range(8)]

        early_sb = sb("early_sb", [P, early_n])
        late_sb = sb("late_sb", [P, late_n])
        ffn_sb = sb("ffn_sb", [P, ffn_n])

        def view(tile, table):
            return {k: tile[0:r, a:b] for k, (r, a, b) in table.items()}

        K = view(early_sb, early_at) | view(late_sb, late_at) | view(ffn_sb, ffn_at)
        ones = sb("ones", [P, 512])
        invpos = sb("invpos", [P, L])
        w_mean = sb("w_mean", [D + 1, 2])
        w1ac = sb("w1ac", [D + 1, D])
        w1bc = sb("w1bc", [D, D])
        tables = sb("tables", [ATOMS, 2 * D])
        half_pi = sb("half_pi", [P, 1])
        wk_bd = sb("wk_bd", [P, P])
        ksk_bias = sb("ksk_bias", [P, 1])
        outw_g = sb("outw_g", [P, P])
        row_bias = sb("row_bias", [P, D])
        NA = NC * PH + W
        ang = sb("ang", [P, NA])
        ang_n = sb("ang_n", [P, NA])
        ang_abs = sb("ang_abs", [P, NA])
        ang_sin = sb("ang_sin", [P, NA])
        ang_cos = sb("ang_cos", [P, NA])
        turn = sb("turn", [P, NC, PH])
        d_exp = sb("d_exp", [P, W])
        w1hi = sb("w1hi", [P, E * HID], F32R)
        w1lo = sb("w1lo", [D + MASK_ROWS, E * HID], F32R)

        onehot = sb("onehot", [ATOMS, B * L])
        neigh = sb("neigh", [P, B, NC, D])
        dist_sb = sb("dist_sb", [P, 2, NC, L])
        mask_in = sb("mask_in", [P, B, NC, L // 4], I32)
        mask_sb = mask_in[:, :, :, :].bitcast(U8)
        wm = sb("wm", [P, 2, NC, L])
        h1_t = sb("h1_t", [P, L])
        sq = sb("sq", [P, 512])
        hn = sb("hn", [P, NC, NH_, D])
        f_t = sb("f_t", [P, L])
        h = sb("h", [P, NG, NC, NH_, D])
        hc = sb("hc", [P, NC, NH_, D])
        x = sb("x", [P, NG, NC, NH_, D])
        st_sum = sb("st_sum", [P, 8])
        st_r = sb("st_r", [P, 8])
        rs_v = sb("rs_v", [P, 40])
        rs_a = sb("rs_a", [P, 40])
        rs_y = sb("rs_y", [P, 40])

        x_t = sb("x_t", [P, L])
        cx = sb("cx", [P, L])
        hop_g = sb("hop_g", [P, L])
        ksk_g = sb("ksk_g", [P, L])
        sg_g = sb("sg_g", [2 * SGH, L])
        vk = sb("vk", [P, NG, NC, VK])
        kph = sb("kph", [P, NG, 2, 8, PH])
        kph_abs = sb("kph_abs", [P, 2, 8, PH])
        t_c = sb("t_c", [P, NG, 8, H * PH])
        zg = sb("zg", [P, NG, 40])
        tg = sb("tg", [P, NG, 40])
        gate = sb("gate", [P, NG, 8])
        gsum = sb("gsum", [P, NG, 8])

        wexp = sb("wexp", [P, 32, W])
        wtmp = sb("wtmp", [P, 32, W])
        wden = sb("wden", [P, 32])
        csum = sb("csum", [P, 2, 32])
        wscr = sb("wscr", [P, 5, 32])
        gcr = sb("gcr", [P, 8])
        phi = sb("phi", [P, 32])
        mag = sb("mag", [P, 32])
        th = sb("th", [P, 8, H * PH])
        thn = sb("thn", [P, 8, H * PH])
        q_sc = sb("q_sc", [P, 2, 8, H * PH])
        ids_sb = q_sc[0:ATOMS, :, :, :].rearrange("p k t l -> p (k t l)").bitcast(I32)
        feat = sb("feat", [P, NG, 2, 8, P])

        wm_flat = wm[:, :, :, :].rearrange("p a c l -> p (a c l)")
        q_t = wm_flat[:, 0:1024].rearrange("p (c f i) -> p c f i", f=NH_, i=P)
        k_t = wm_flat[:, 1024:2048].rearrange("p (c f i) -> p c f i", f=NH_, i=P)
        s_m = wm_flat[:, 2048:3072].rearrange("p (a k f i) -> p a k f i", a=2, k=2, i=P)
        state = sb("state", [P, 3, P])
        comb = sb("comb", [P, NC, NH_, D])
        sq_c = sb("sq_c", [P, 512])
        cc_t = sb("cc_t", [P, L])
        h3 = sb("h3", [P, NG, NC, NH_, D])

        xhl = sb("xhl", [P, 8, 2 * D + D // 2], F32R)
        x2 = hc
        xp1 = sb("xp1", [P, 8 * P], F32R)
        xp2 = sb("xp2", [D + MASK_ROWS, 8 * P], F32R)
        score = sb("score", [P, 8, E])
        sel = sb("sel", [P, 8, E])
        sel2 = sb("sel2", [P, 8, E])
        best = sb("best", [P, 8])
        dist_flat = dist_sb[:, :, :, :].rearrange("p a c l -> p (a c l)")
        mrow_in = dist_flat[0:D + MASK_ROWS, 0:1024]
        mrow_lo = dist_flat[0:D + MASK_ROWS, 1024:2048]
        hid = dist_flat[:, 2048:2048 + 3 * 512].rearrange("p (s l) -> p s l", s=3)
        y_t = dist_flat[:, 2048 + 3 * 512:4096]

        early_in, ids_in, late_in, ffn_in = sem("early_in"), sem("ids_in"), sem("late_in"), sem("ffn_in")
        dist_in = [sem(f"dist_in{b}") for b in range(B)]
        stored = sem("stored")
        dve_step, pool_step = sem("dve_step"), sem("pool_step")
        names = """ones_set w1_centred tables_mm tables_set onehot_set neigh_mm neigh_set wm_zero diag_off
            dist_masked h1_mm h1_copied h1t_mm h1_sq h1_norm hn_mm f_set h2_mm h_set x_centred x_sq x_set
            trig_abs trig_set kang_set fold_mm fold_set fused_set
            xt_mm xt_set cx_set hop_mm hop_set sg_mm sg_set vk_mm vk_set z_mm zg_set tg_set ksk_mm ksk_set
            center_mm center_set center_tanh st_mm st_set kq_tanh st_tanh gate_set gate_mm gate_read
            w_pre w_exp at_arg at_set kph_abs_set k_feat th_set tha_set sin_set cos_set q_sum 
            ktr_mm ktr_set qtr_mm qtr_set s_mm s_masked state_mm state_set out_mm comb_centred comb_sq
            cct_mm cct_set attn_mm h3_set hx_set
            x2_centred x2_sq xhl_set xp1_mm xp1_set score_mm score_read mask_set xp2_mm xp2_set w1_hi w1_lo
            hid_mm hid_set y_mm y_copied yt_mm y_set""".split()
        S = {n: sem(n) for n in names}
        block = ctx.enter_context(nc.Block())

        def v8(t):
            return t.rearrange("p c f d -> p (c f) d")

        def bc(t, n):
            return t.unsqueeze(2).broadcast_to([P, t.shape[1], n])

        def rows_bc(t, n):
            return t.unsqueeze(1).broadcast_to([P, n, t.shape[1]])

        def b3(i):
            return bank[i][:, :].rearrange("p (t d) -> p t d", d=D)

        def pair(t, c):
            return t[:, c, :, :].rearrange("p f d -> p (f d)")

        def flat(t):
            return t.rearrange("p a b -> p (a b)")

        def values(g):
            return vk[:, g, :, 2 * D:4 * D].rearrange("p c (f d) -> p c f d", d=D)

        @block.sync
        def _(sp):
            sp.dma_start(early_sb[:, :], early).then_inc(early_in, 16)
            sp.dma_start(ids_sb, ids.broadcast_to([ATOMS, B * L])).then_inc(ids_in, 16)

            def load(b):
                if b >= 2:
                    sp.wait_ge(S["dist_masked"], 2 * (b - 1))
                sp.dma_start(mask_in[:, b], mask[b].rearrange("(c p) j -> p c j", p=P)).then_inc(dist_in[b], 16)
                sp.dma_start(dist_sb[:, b % 2], dist[b].rearrange("(c p) j -> p c j", p=P)).then_inc(dist_in[b], 16)

            load(0)
            load(1)
            sp.dma_start(late_sb[:, :], late).then_inc(late_in, 16)
            load(2)
            load(3)
            sp.dma_start(ffn_sb[:, :], ffn).then_inc(ffn_in, 16)
            sp.wait_ge(S["dist_masked"], 2 * B)
            sp.dma_start(mrow_in[D:D + MASK_ROWS, :], mrows).then_inc(ffn_in, 16)
            for g in range(NG):
                for f in range(NH_):
                    sp.wait_ge(S["y_set"], g + 1)
                    sp.dma_start(out[2 * g + f].rearrange("(c p) d -> p c d", p=P),
                                 h[:, g, :, f]).then_inc(stored, 16)
            sp.wait_ge(stored, 16 * B)

        @block.gpsimd
        def _(pool):
            nc.gpsimd.memset(wm[:, 0, 0:2], 0.0).then_inc(S["wm_zero"], 1)
            nc.gpsimd.memset(wm[:, 0, 2:4], 0.0).then_inc(S["wm_zero"], 1)
            nc.gpsimd.memset(ones[:, :], 1.0).then_inc(S["ones_set"], 1)
            nc.gpsimd.memset(half_pi[:, :], PI / 2).then_inc(S["ones_set"], 1)
            nc.gpsimd.iota(invpos[:, :], [[1, L]], base=1, channel_multiplier=0,
                           allow_small_or_imprecise_dtypes=True).then_inc(S["ones_set"], 1)
            nc.gpsimd.memset(xhl[:, :, 2 * D + 16:2 * D + 18].bitcast(F32), 1.0).then_inc(S["ones_set"], 1)
            nc.gpsimd.memset(xhl[:, :, 2 * D + 18:].bitcast(F32), 0.0).then_inc(S["ones_set"], 1)
            for b in range(B):
                if b >= 2:
                    pool.wait_ge(S["h1_mm"], b - 1)
                if b:
                    for k in range(2):
                        nc.gpsimd.memset(wm[:, b % 2, 2 * k:2 * k + 2], 0.0).then_inc(S["wm_zero"], 1)
                pool.wait_ge(dist_in[b], 32)
                for c in range(NC):
                    diag = mask_sb[:, b, c, c * P:(c + 1) * P].bitcast(I8)
                    nc.gpsimd.affine_select(out=diag, in_=diag, compare_op=ALU.not_equal, fill=0.0, base=0,
                                            pattern=[[-1, P]], channel_multiplier=1).then_inc(S["diag_off"], 1)
            pool.wait_ge(S["trig_set"], 2)
            for g in range(NG):
                for f in range(NH_):
                    for k, trig in ((0, ang_cos), (1, ang_sin)):
                        dst = feat[:, g, 1, :, k * PH:(k + 1) * PH].rearrange("p (c f) q -> p c f q", f=2)[:, :, f]
                        nc.gpsimd.tensor_copy(dst, trig[:, 0:NC * PH].rearrange("p (c q) -> p c q", q=PH)
                                              ).then_inc(S["kang_set"], 1)
            for g in range(NG):
                pool.wait_ge(S["fused_set"], 1)
                pool.wait_ge(S["x_set"], g + 1)
                pool.wait_ge(S["xt_mm"], g + 1)
                nc.gpsimd.tensor_tensor(v8(x[:, g]), v8(h[:, g]), v8(x[:, g]), ALU.add).then_inc(pool_step, 1)
                pool.wait_ge(pool_step, g + 1)
                nc.gpsimd.tensor_tensor(v8(x[:, g]), v8(x[:, g]), rows_bc(row_bias[:, :], 8),
                                        ALU.add).then_inc(S["hx_set"], 1)

        @block.scalar
        def _(act):
            def token(g):
                if g == 0:
                    for n, i in ((0, 5), (1, 7)):
                        act.wait_ge(S["neigh_mm"], n + 1)
                        nc.scalar.copy(neigh[:, 2 * n:2 * n + 2].rearrange("p b c d -> p (b c) d"),
                                       b3(i)).then_inc(S["neigh_set"], 1)
                yield
                yield
                act.wait_ge(S["h1_mm"], 2 * g + 2)
                if g:
                    act.wait_ge(S["h1t_mm"], g)
                nc.scalar.copy(h1_t[:, :], bank[4][:, :]).then_inc(S["h1_copied"], 1)
                yield
                act.wait_ge(S["h1t_mm"], g + 1)
                if g:
                    act.wait_ge(S["x_set"], g)
                nc.scalar.activation(sq[:, :], bank[6][:, :], ACT.Square).then_inc(S["h1_sq"], 1)
                yield
                act.wait_ge(S["hn_mm"], g + 1)
                if g:
                    act.wait_ge(S["h2_mm"], g)
                nc.scalar.activation(f_t[:, :], bank[7][:, :], ACT.Silu, bias=K["beta"],
                                     scale=K["gamma"]).then_inc(S["f_set"], 1)
                yield
                act.wait_ge(S["x_centred"], g + 1)
                nc.scalar.activation(sq[:, :], hc[:].rearrange("p c f d -> p (c f d)"),
                                     ACT.Square).then_inc(S["x_sq"], 1)
                if g == 0:
                    act.wait_ge(S["ones_set"], 5)
                    act.wait_ge(S["trig_abs"], 1)
                    nc.scalar.activation(ang_sin[:, :], ang[:, :], ACT.Sin).then_inc(S["trig_set"], 1)
                    nc.scalar.activation(ang_cos[:, :], ang_abs[:, :], ACT.Sin, bias=half_pi[:, :],
                                         scale=-1.0).then_inc(S["trig_set"], 1)
                yield

            def project(g):
                act.wait_ge(S["xt_mm"], g + 1)
                if g:
                    act.wait_ge(S["vk_mm"], NC * g)
                    act.wait_ge(S["ksk_mm"], g)
                nc.scalar.copy(x_t[:, :], bank[0][:, :]).then_inc(S["xt_set"], 1)
                yield
                act.wait_ge(S["hop_mm"], g + 1)
                if g:
                    act.wait_ge(S["center_mm"], 2 * g)
                nc.scalar.activation(hop_g[:, :], bank[1][:, :], ACT.Gelu, bias=K["hop_b1"]).then_inc(S["hop_set"], 1)
                act.wait_ge(S["sg_mm"], g + 1)
                nc.scalar.activation(sg_g[:, :], bank[2][0:2 * SGH, :], ACT.Gelu,
                                     bias=K["sg_b1"]).then_inc(S["sg_set"], 1)
                yield
                act.wait_ge(S["ksk_mm"], g + 1)
                act.wait_ge(S["fold_set"], 1)
                if g:
                    act.wait_ge(S["st_mm"], g)
                nc.scalar.activation(ksk_g[:, :], bank[2][:, :], ACT.Gelu,
                                     bias=ksk_bias[:, :]).then_inc(S["ksk_set"], 1)
                act.wait_ge(S["zg_set"], g + 1)
                nc.scalar.activation(tg[:, g], zg[:, g], ACT.Tanh, scale=0.5).then_inc(S["tg_set"], 1)
                yield
                act.wait_ge(S["vk_set"], NC * (g + 1))
                nc.scalar.activation(kph[:, g, 0].rearrange("p (c f) q -> p c (f q)", f=2), vk[:, g, :, 4 * D:VK],
                                     ACT.Tanh).then_inc(S["kq_tanh"], 1)
                for k in range(2):
                    act.wait_ge(S["center_set"], 2 * g + k + 1)
                    half = flat(t_c[:, g, 4 * k:4 * k + 4])
                    nc.scalar.activation(half, half, ACT.Tanh).then_inc(S["center_tanh"], 1)
                act.wait_ge(S["st_set"], g + 1)
                nc.scalar.activation(kph[:, g, 1], kph[:, g, 1], ACT.Tanh).then_inc(S["st_tanh"], 1)
                yield

            def queries(g):
                act.wait_ge(S["w_pre"], g + 1)
                nc.scalar.activation(wexp[:], wexp[:], ACT.Exp).then_inc(S["w_exp"], 1)
                yield
                act.wait_ge(S["kph_abs_set"], g + 1)
                for k in range(2):
                    for n, src, bias, scale in ((3, kph[:, g, k], None, TWO_PI / 2), (2, kph_abs[:, k], half_pi, -TWO_PI / 2)):
                        ins = nc.scalar.activation(feat[:, g, k, :, n * PH:(n + 1) * PH], src, ACT.Sin, scale=scale,
                                                   **({"bias": bias[:, :]} if bias is not None else {}))
                    ins.then_inc(S["k_feat"], 1)
                act.wait_ge(S["at_arg"], g + 1)
                nc.scalar.activation(wscr[:, 3], wscr[:, 2], ACT.Arctan).then_inc(S["at_set"], 1)
                yield
                for k in range(2):
                    act.wait_ge(S["th_set"], 2 * g + k + 1)
                    if g:
                        act.wait_ge(S["q_sum"], 2 * g)
                    nc.scalar.activation(q_sc[:, 1, 4 * k:4 * k + 4], th[:, 4 * k:4 * k + 4], ACT.Sin,
                                         scale=TWO_PI).then_inc(S["sin_set"], 1)
                    act.wait_ge(S["tha_set"], 2 * g + k + 1)
                    nc.scalar.activation(q_sc[:, 0, 4 * k:4 * k + 4], thn[:, 4 * k:4 * k + 4], ACT.Sin,
                                         bias=half_pi[:, :], scale=-TWO_PI).then_inc(S["cos_set"], 1)
                yield
                yield

            def chunks(g):
                for k in range(2):
                    act.wait_ge(S["ktr_mm"], 2 * g + k + 1)
                    if g:
                        act.wait_ge(S["out_mm"], NC * g)
                    nc.scalar.copy(k_t[:, 2 * k:2 * k + 2].rearrange("p c f i -> p (c f i)"),
                                   bank[4 + k][:, :]).then_inc(S["ktr_set"], 1)
                yield
                for k in range(2):
                    act.wait_ge(S["qtr_mm"], 2 * g + k + 1)
                    nc.scalar.copy(q_t[:, 2 * k:2 * k + 2].rearrange("p c f i -> p (c f i)"),
                                   bank[6 + k][:, :]).then_inc(S["qtr_set"], 1)
                yield
                yield
                yield
                yield
                yield
                act.wait_ge(S["comb_centred"], g + 1)
                nc.scalar.activation(sq_c[:, :], comb[:].rearrange("p c f d -> p (c f d)"),
                                     ACT.Square).then_inc(S["comb_sq"], 1)
                yield
                act.wait_ge(S["cct_mm"], g + 1)
                nc.scalar.copy(cc_t[:, :], bank[4][:, :]).then_inc(S["cct_set"], 1)
                yield

            def experts(g):
                if g == 0:
                    act.wait_ge(ffn_in, 32)
                    nc.scalar.copy(w1hi[:, :], K["e_w1"]).then_inc(S["w1_hi"], 1)
                    nc.scalar.copy(w1lo[D:D + MASK_ROWS, :], mrow_in[D:D + MASK_ROWS, :]).then_inc(S["w1_hi"], 1)
                act.wait_ge(S["x2_centred"], g + 1)
                nc.scalar.activation(sq[:, :], x2[:].rearrange("p c f d -> p (c f d)"),
                                     ACT.Square).then_inc(S["x2_sq"], 1)
                yield
                if g:
                    act.wait_ge(S["hid_mm"], 16 * g)
                for k in range(2):
                    act.wait_ge(S["xp1_mm"], 2 * g + k + 1)
                    nc.scalar.copy(xp1[:, 512 * k:512 * k + 512], bank[k][:, :]).then_inc(S["xp1_set"], 1)
                yield
                for k in range(2):
                    act.wait_ge(S["xp2_mm"], 2 * g + k + 1)
                    nc.scalar.copy(xp2[:, 512 * k:512 * k + 512], bank[k][0:D + MASK_ROWS, :]).then_inc(S["xp2_set"], 1)
                yield
                for n in range(16):
                    act.wait_ge(S["hid_mm"], 16 * g + n + 1)
                    if n >= 3 or g:
                        act.wait_ge(S["y_mm"], 16 * g + n - 2)
                    nc.scalar.activation(hid[:, (16 * g + n) % 3], bank[n % 2][:, :],
                                         ACT.Gelu).then_inc(S["hid_set"], 1)
                    yield
                for k in range(2):
                    act.wait_ge(S["y_mm"], 16 * g + 8 * k + 8)
                    rows = slice(k * D, (k + 1) * D)
                    nc.scalar.copy(y_t[rows, :], bank[2 + k][rows, :]).then_inc(S["y_copied"], 1)
                yield

            follow({"T": token, "P": project, "Q": queries, "C": chunks, "X": experts})

        @block.tensor
        def _(pe):
            ident = K["ident"]

            def token(g):
                if g == 0:
                    pe.wait_ge(S["w1_centred"], 2)
                    nc.tensor.matmul(bank[6][0:ATOMS, 0:D], K["atom_T1"], w1ac[:, :], start=True, stop=True)
                    nc.tensor.matmul(bank[6][0:ATOMS, D:2 * D], K["neigh_T"], w1bc[:, :], start=True,
                                     stop=True).then_inc(S["tables_mm"], 1)
                    pe.wait_ge(S["tables_set"], 1)
                    pe.wait_ge(S["onehot_set"], 4)
                    for n, i in ((0, 5), (1, 7)):
                        for t in range(8):
                            at = (8 * n + t) * P
                            mm = nc.tensor.matmul(b3(i)[:, t], onehot[:, at:at + P], tables[:, D:2 * D], start=True, stop=True)
                        mm.then_inc(S["neigh_mm"], 1)
                yield
                for f in range(NH_):
                    b = 2 * g + f
                    rows = bank[4][f * D:(f + 1) * D, :]
                    if f == 0:
                        pe.wait_ge(S["neigh_set"], g + 1)
                        if g:
                            pe.wait_ge(S["h1_copied"], g)
                    nc.tensor.matmul(rows, tables[:, 0:D], onehot[:, b * L:(b + 1) * L], start=True, stop=False)
                    for j in range(NC):
                        if j % 2 == 0:
                            pe.wait_ge(S["dist_masked"], 2 * b + j // 2 + 1)
                        mm = nc.tensor.matmul(rows, neigh[:, b, j], wm[:, b % 2, j], start=False, stop=(j == NC - 1))
                    mm.then_inc(S["h1_mm"], 1)
                    if f == 0:
                        yield
                yield
                pe.wait_ge(S["h1_copied"], g + 1)
                if g:
                    pe.wait_ge(S["h1_norm"], g)
                for c in range(NC):
                    mm = nc.tensor.transpose(bank[6][:, c * P:(c + 1) * P], h1_t[:, c * P:(c + 1) * P], ident)
                mm.then_inc(S["h1t_mm"], 1)
                yield
                pe.wait_ge(S["h1_norm"], g + 1)
                pe.wait_ge(S["f_set"], g) if g else pe.wait_ge(S["neigh_set"], 2)
                for c in range(NC):
                    mm = nc.tensor.transpose(bank[7][:, c * P:(c + 1) * P], pair(hn, c), ident)
                mm.then_inc(S["hn_mm"], 1)
                yield
                pe.wait_ge(S["f_set"], g + 1)
                if g:
                    pe.wait_ge(S["h_set"], g)
                for c in range(NC):
                    mm = nc.tensor.matmul(bank[5][:, c * P:(c + 1) * P], f_t[:, c * P:(c + 1) * P], K["w2_bd"],
                                          start=True, stop=True)
                mm.then_inc(S["h2_mm"], 1)
                if g == 0:
                    pe.wait_ge(late_in, 16)
                    nc.tensor.matmul(bank[3][:, 0:P], K["kce_T_bd"], K["ksk1c_bd"], start=True, stop=True)
                    nc.tensor.matmul(bank[3][:, P:P + 1], K["ksk1c_dup"], K["kce_b"], start=True, stop=True)
                    nc.tensor.matmul(bank[3][:, P + 64:P + 64 + D], K["ln_b"], K["out_w"], start=True,
                                     stop=True).then_inc(S["fold_mm"], 1)
                yield

            def project(g):
                pe.wait_ge(S["x_set"], g + 1)
                if g:
                    pe.wait_ge(S["gate_read"], g)
                for c in range(NC):
                    mm = nc.tensor.transpose(bank[0][:, c * P:(c + 1) * P], pair(x[:, g], c), ident)
                mm.then_inc(S["xt_mm"], 1)
                yield
                pe.wait_ge(S["xt_set"], g + 1)
                if g:
                    pe.wait_ge(S["st_set"], g)
                nc.tensor.matmul(bank[1][:, :], K["hop1x_bd"], x_t[:, :], start=True, stop=False)
                nc.tensor.matmul(bank[1][:, :], K["hop1p"], K["pp_T"], start=False, stop=True).then_inc(S["hop_mm"], 1)
                if g:
                    pe.wait_ge(S["center_set"], 2 * g)
                nc.tensor.matmul(bank[2][0:2 * SGH, :], K["sg1_bd"], x_t[:, :], start=True,
                                 stop=True).then_inc(S["sg_mm"], 1)
                pe.wait_ge(S["fold_set"], 1)

                def joint(c, i):
                    nc.tensor.matmul(bank[i][:, 0:VK], x_t[:, c * P:(c + 1) * P], K["vk_bd"], start=True,
                                     stop=True).then_inc(S["vk_mm"], 1)

                joint(0, 3)
                joint(1, 0)
                yield
                pe.wait_ge(S["hop_set"], g + 1)
                for c in range(NC):
                    nc.tensor.matmul(bank[1][:, c * 8:(c + 1) * 8], hop_g[:, c * P:(c + 1) * P], K["hop2w_bd"],
                                     start=True, stop=True)
                pe.wait_ge(S["sg_set"], g + 1)
                for c in range(NC):
                    mm = nc.tensor.matmul(bank[1][:, 32 + c * 2:34 + c * 2], sg_g[:, c * P:(c + 1) * P], K["sg2_bd"],
                                          start=True, stop=True)
                mm.then_inc(S["z_mm"], 1)
                nc.tensor.matmul(bank[2][:, :], K["ksk1x_bd"], x_t[:, :], start=True, stop=False)
                pe.wait_ge(S["cx_set"], g + 1)
                nc.tensor.matmul(bank[2][:, :], wk_bd[:, :], cx[:, :], start=False, stop=True).then_inc(S["ksk_mm"], 1)
                for c, i in ((2, 3), (3, 0)):
                    pe.wait_ge(S["vk_set"], NC * g + c - 1)
                    joint(c, i)
                yield

                def center(k, i):
                    for c in (0, 1):
                        mm = nc.tensor.matmul(bank[i][:, c * 256:(c + 1) * 256],
                                              hop_g[:, (2 * k + c) * P:(2 * k + c + 1) * P], K["hop2c_bd"],
                                              start=True, stop=True)
                    mm.then_inc(S["center_mm"], 1)

                pe.wait_ge(S["ksk_set"], g + 1)
                center(0, 2)
                pe.wait_ge(S["vk_set"], NC * g + 3)
                center(1, 3)
                pe.wait_ge(S["zg_set"], g + 1)
                for c in range(NC):
                    mm = nc.tensor.matmul(bank[1][:, c * 64:(c + 1) * 64], ksk_g[:, c * P:(c + 1) * P], K["ksk2_bd"],
                                          start=True, stop=True)
                mm.then_inc(S["st_mm"], 1)
                pe.wait_ge(S["vk_set"], NC * g + 4)
                pe.wait_ge(S["gate_set"], g + 1)
                nc.tensor.matmul(bank[0][:, 0:8], K["tri"], gate[:, g], start=True, stop=True)
                for n in range(1, NC):
                    mm = nc.tensor.matmul(bank[0][:, 2 * n:8], ones[:, 0:P], gate[:, g, 0:8 - 2 * n], start=False,
                                          stop=True, skip_group_check=True)
                mm.then_inc(S["gate_mm"], 1)
                yield

            def queries(g):
                for _ in range(4):
                    yield

            def chunks(g):
                pe.wait_ge(S["k_feat"], 2 * g + 2)
                pe.wait_ge(S["kang_set"], 8)
                if g == 0:
                    pe.wait_ge(S["h_set"], NG)
                pe.wait_ge(S["h3_set"], g) if g else pe.wait_ge(S["h1_copied"], NG)
                if g:
                    pe.wait_ge(S["cct_set"], g)
                for k in range(2):
                    for t in range(4):
                        mm = nc.tensor.transpose(bank[4 + k][:, t * P:(t + 1) * P], feat[:, g, 1, 4 * k + t], ident)
                    mm.then_inc(S["ktr_mm"], 1)
                yield
                pe.wait_ge(S["q_sum"], 2 * g + 2)
                if g:
                    pe.wait_ge(S["state_set"], 3 * g)
                    pe.wait_ge(S["comb_centred"], g)
                else:
                    pe.wait_ge(S["h1_norm"], NG)
                    pe.wait_ge(S["f_set"], NG)
                for k in range(2):
                    for t in range(4):
                        mm = nc.tensor.transpose(bank[6 + k][:, t * P:(t + 1) * P], feat[:, g, 0, 4 * k + t], ident)
                    mm.then_inc(S["qtr_mm"], 1)
                yield

                def scores(c):
                    at = g * NC + c
                    pe.wait_ge(S["qtr_set"], 2 * g + c // 2 + 1)
                    pe.wait_ge(S["ktr_set"], 2 * g + 2)
                    if c:
                        pe.wait_ge(S["s_masked"], 2 * at - 1)
                    lo, hi = slice(0, D), slice(D, P)
                    nc.tensor.matmul(bank[4][:, 0:2 * P], k_t[lo, c, 0], q_t[lo, c].rearrange("p f i -> p (f i)"),
                                     start=True, stop=True).then_inc(S["s_mm"], 1)
                    if c:
                        pe.wait_ge(S["s_masked"], 2 * at)
                    for f in range(NH_):
                        mm = nc.tensor.matmul(bank[5][:, f * P:(f + 1) * P], k_t[hi, c, f], q_t[hi, c, f], start=True, stop=True)
                    mm.then_inc(S["s_mm"], 1)

                def chunk_state(c):
                    pe.wait_ge(S["state_set"], 3 * g + c) if c else pe.wait_ge(S["qtr_set"], 2 * g + 1)
                    nc.tensor.matmul(bank[6][0:D, 0:P], feat[:, g, 1, 2 * c, 0:D], vk[:, g, c, 0:P], start=True, stop=True)
                    for f in range(NH_):
                        mm = nc.tensor.matmul(bank[6][D:P, f * D:(f + 1) * D], feat[:, g, 1, 2 * c + f, D:P],
                                              values(g)[:, c, f], start=True, stop=True)
                    mm.then_inc(S["state_mm"], 1)

                def outputs(c):
                    if c == 0:
                        pe.wait_ge(S["qtr_set"], 2 * g + 2)
                    pe.wait_ge(S["s_masked"], 2 * (g * NC + c + 1))
                    if c:
                        pe.wait_ge(S["state_set"], 3 * g + c)
                    for f in range(NH_):
                        o = b3(7)[:, 2 * c + f]
                        nc.tensor.matmul(o, s_m[:, c % 2, 0, f], vk[:, g, c, f * D:(f + 1) * D], start=True, stop=False)
                        mm = nc.tensor.matmul(o, s_m[:, c % 2, 1, f], values(g)[:, c, f], start=False, stop=(c == 0))
                        if c:
                            mm = nc.tensor.matmul(o, q_t[:, c, f], state[:, c - 1, f * D:(f + 1) * D], start=False, stop=True)
                    mm.then_inc(S["out_mm"], 1)

                scores(0)
                yield
                for c in range(NC):
                    if c + 1 < NC:
                        scores(c + 1)
                        chunk_state(c)
                    outputs(c)
                    if c < NC - 1:
                        yield
                yield
                pe.wait_ge(S["comb_centred"], g + 1)
                pe.wait_ge(S["s_masked"], 2 * NC * (g + 1))
                for c in range(NC):
                    mm = nc.tensor.transpose(bank[4][:, c * P:(c + 1) * P], pair(comb, c), ident)
                mm.then_inc(S["cct_mm"], 1)
                pe.wait_ge(S["cct_set"], g + 1)
                for c in range(NC):
                    mm = nc.tensor.matmul(bank[5][:, c * P:(c + 1) * P], cc_t[:, c * P:(c + 1) * P], outw_g[:, :],
                                          start=True, stop=True)
                mm.then_inc(S["attn_mm"], 1)
                yield

            def experts(g):
                yield
                pe.wait_ge(S["xhl_set"], g + 1)
                if g == 0:
                    pe.wait_ge(S["gate_read"], NG)
                    pe.wait_ge(S["st_set"], NG)
                else:
                    pe.wait_ge(S["hid_set"], 16 * g)
                    pe.wait_ge(S["y_set"], g)
                f32 = xhl[:].bitcast(F32)
                for n in range(2):
                    for t in range(4):
                        mm = nc.tensor.transpose(bank[n][:, t * P:(t + 1) * P], f32[:, 4 * n + t, 0:2 * D], ident)
                    mm.then_inc(S["xp1_mm"], 1)
                pe.wait_ge(S["xp1_set"], 2 * g + 2)
                pe.wait_ge(S["y_copied"], 2 * g) if g else pe.wait_ge(S["center_set"], 2 * NG)
                for t in range(8):
                    mm = nc.tensor.matmul(bank[3][:, t * E:(t + 1) * E], xp1[:, t * P:(t + 1) * P].bitcast(F32), K["wg"],
                                          start=True, stop=True)
                mm.then_inc(S["score_mm"], 1)
                yield
                pe.wait_ge(S["mask_set"], g + 1)
                for n in range(2):
                    for t in range(4):
                        mm = nc.tensor.transpose(bank[n][0:D + MASK_ROWS, t * P:(t + 1) * P],
                                                 f32[:, 4 * n + t, D:2 * D + MASK_ROWS], ident)
                    mm.then_inc(S["xp2_mm"], 1)
                yield
                pe.wait_ge(S["xp2_set"], 2 * g + 2)
                pe.wait_ge(S["w1_hi"], 2)
                pe.wait_ge(S["w1_lo"], 2)
                pe.wait_ge(S["score_read"], g + 1)

                def hidden(n):
                    k, e = n // E, n % E
                    if n >= 2:
                        pe.wait_ge(S["hid_set"], 16 * g + n - 1)
                    toks = slice(k * 512, (k + 1) * 512)
                    nc.tensor.matmul(bank[n % 2][:, :], w1hi[:, e * HID:(e + 1) * HID], xp1[:, toks],
                                     start=True, stop=False)
                    nc.tensor.matmul(bank[n % 2][:, :], w1lo[:, e * HID:(e + 1) * HID], xp2[:, toks],
                                     start=False, stop=True).then_inc(S["hid_mm"], 1)

                def back(n):
                    k, e = n // E, n % E
                    y = bank[2 + k][k * D:(k + 1) * D, :]
                    if e == 0:
                        nc.tensor.matmul(y, K["e_b2"][D:D + MASK_ROWS, :],
                                         xp2[D:D + MASK_ROWS, k * 512:(k + 1) * 512].bitcast(F32),
                                         start=True, stop=False)
                    pe.wait_ge(S["hid_set"], 16 * g + n + 1)
                    nc.tensor.matmul(y, K["e_w2"][:, e * D:(e + 1) * D], hid[:, (16 * g + n) % 3],
                                     start=False, stop=(e == E - 1)).then_inc(S["y_mm"], 1)

                hidden(0)
                for n in range(16):
                    if n + 1 < 16:
                        hidden(n + 1)
                    back(n)
                    yield
                pe.wait_ge(S["y_copied"], 2 * g + 2)
                for c in range(4):
                    mm = nc.tensor.transpose(bank[0][:, c * P:(c + 1) * P], y_t[:, c * P:(c + 1) * P], ident)
                mm.then_inc(S["yt_mm"], 1)
                yield

            follow({"T": token, "P": project, "Q": queries, "C": chunks, "X": experts})

        @block.vector
        def _(dve):
            steps = [0]

            def link(ins):
                steps[0] += 1
                ins.then_inc(dve_step, 1)
                dve.wait_ge(dve_step, steps[0])

            def magnitude(dst, src):
                return nc.vector.tensor_scalar(dst.bitcast(I32), src.bitcast(I32), 0x7FFFFFFF, None, ALU.bitwise_and)

            def rsqrt(out_ap, n):
                v, a, y = rs_v[:, 0:n], rs_a[:, 0:n], rs_y[:, 0:n]
                link(nc.vector.tensor_scalar(a.bitcast(I32), v.bitcast(I32), 1, None, ALU.logical_shift_right))
                link(nc.vector.tensor_scalar(y.bitcast(I32), a.bitcast(I32), -1.0, float(0x5F3759DF), ALU.mult, ALU.add))
                for i in range(3):
                    link(nc.vector.tensor_tensor(a, y, y, ALU.mult))
                    link(nc.vector.scalar_tensor_tensor(out=a, in0=a, scalar=-0.5, in1=v, op0=ALU.mult, op1=ALU.mult))
                    link(nc.vector.scalar_tensor_tensor(out=out_ap if i == 2 else y, in0=a, scalar=1.5, in1=y,
                                                        op0=ALU.add, op1=ALU.mult))

            def variance(squares):
                link(nc.vector.tensor_reduce(st_sum[:, :], squares[:, :].rearrange("p (t d) -> p t d", d=D), AX_X, ALU.add))
                link(nc.vector.tensor_scalar(rs_v[:, 0:8], st_sum[:, :], 1.0 / D, EPS, ALU.mult, ALU.add))

            def centre(dst, src, done):
                link(nc.vector.tensor_reduce(st_sum[:, :], src, AX_X, ALU.add))
                link(nc.vector.tensor_scalar(st_sum[:, :], st_sum[:, :], -1.0 / D, None, ALU.mult))
                nc.vector.tensor_tensor(dst, src, bc(st_sum[:, :], D), ALU.add).then_inc(S[done], 1)

            def tok_tables():
                dve.wait_ge(early_in, 16)
                nc.vector.tensor_reduce(w_mean[:, 0:1], K["w1a_b1"], AX_X, ALU.add)
                link(nc.vector.tensor_reduce(w_mean[0:D, 1:2], K["w1b"], AX_X, ALU.add))
                link(nc.vector.tensor_scalar(w_mean[:, 0:1], w_mean[:, 0:1], -1.0 / D, None, ALU.mult))
                link(nc.vector.tensor_scalar(w_mean[0:D, 1:2], w_mean[0:D, 1:2], -1.0 / D, None, ALU.mult))
                nc.vector.tensor_scalar(w1ac[:, :], K["w1a_b1"], w_mean[:, 0:1], None, ALU.add).then_inc(S["w1_centred"], 1)
                nc.vector.tensor_scalar(w1bc[:, :], K["w1b"], w_mean[0:D, 1:2], K["w_rd"], ALU.add,
                                        ALU.mult).then_inc(S["w1_centred"], 1)
                dve.wait_ge(ids_in, 16)
                for n in range(4):
                    nc.vector.tensor_scalar(onehot[:, n * 512:(n + 1) * 512], ids_sb[:, n * 512:(n + 1) * 512],
                                            K["part_id"][0:ATOMS, :], None, ALU.is_equal).then_inc(S["onehot_set"], 1)
                dve.wait_ge(S["tables_mm"], 1)
                nc.vector.tensor_copy(tables[:, :], bank[6][0:ATOMS, 0:2 * D]).then_inc(S["tables_set"], 1)

            def mask_batch(b):
                dve.wait_ge(dist_in[b], 32)
                dve.wait_ge(S["diag_off"], NC * (b + 1))
                dve.wait_ge(S["wm_zero"], 2 * (b + 1))
                for k in range(2):
                    rows = slice(2 * k, 2 * k + 2)
                    nc.vector.copy_predicated(wm[:, b % 2, rows], mask_sb[:, b, rows],
                                              dist_sb[:, b % 2, rows]).then_inc(S["dist_masked"], 1)

            def constants():
                dve.wait_ge(late_in, 16)
                dve.wait_ge(S["ones_set"], 5)
                n2 = NC * PH
                nc.vector.tensor_copy(ang[:, 0:n2], K["pp_tok"])
                link(nc.vector.tensor_scalar(ang[:, n2:], K["deltas"], 0.1, None, ALU.mult))
                link(nc.vector.tensor_scalar(ang_n[:, :], ang[:, :], 1.0 / (2 * np.pi), ROUND, ALU.mult, ALU.add))
                link(nc.vector.tensor_scalar(ang_n[:, :], ang_n[:, :], ROUND, None, ALU.subtract))
                link(nc.vector.scalar_tensor_tensor(out=ang[:, :], in0=ang_n[:, :], scalar=-C1, in1=ang[:, :],
                                                    op0=ALU.mult, op1=ALU.add))
                link(nc.vector.scalar_tensor_tensor(out=ang[:, :], in0=ang_n[:, :], scalar=-C2, in1=ang[:, :],
                                                    op0=ALU.mult, op1=ALU.add))
                link(nc.vector.tensor_scalar(ang[:, :], ang[:, :], TWO_PI / 2, -TWO_PI / 2, ALU.min, ALU.max))
                magnitude(ang_abs[:, :], ang[:, :]).then_inc(S["trig_abs"], 1)
                nc.vector.tensor_scalar(turn[:].rearrange("p c q -> p (c q)"), ang[:, 0:n2], 1.0 / (2 * np.pi), None, ALU.mult)
                link(nc.vector.reciprocal(invpos[:, :], invpos[:, :]))
                link(nc.vector.tensor_tensor(d_exp[:, :], K["deltas"], K["deltas"], ALU.mult))
                link(nc.vector.tensor_scalar(d_exp[:, :], d_exp[:, :], -0.5, None, ALU.mult))
                nc.vector.tensor_scalar(outw_g[:, :], K["out_bd"], K["ln_g"], None, ALU.mult)
                dve.wait_ge(S["fold_mm"], 1)
                nc.vector.tensor_tensor(row_bias[:, :], bank[3][:, P + 64:P + 64 + D], K["out_b"],
                                        ALU.add).then_inc(S["fused_set"], 1)
                nc.vector.tensor_tensor(ksk_bias[:, :], bank[3][:, P:P + 1], K["ksk_b1"], ALU.add)
                nc.vector.tensor_copy(wk_bd[:, :], bank[3][:, 0:P]).then_inc(S["fold_set"], 1)

            def token(g):
                if g == 0:
                    tok_tables()
                mask_batch(2 * g)
                yield
                mask_batch(2 * g + 1)
                yield
                yield
                dve.wait_ge(S["h1_sq"], g + 1)
                variance(sq)
                rsqrt(st_r[:, :], 8)
                nc.vector.tensor_tensor(v8(hn[:]), b3(6), bc(st_r[:, :], D), ALU.mult).then_inc(S["h1_norm"], 1)
                yield
                yield
                dve.wait_ge(S["h2_mm"], g + 1)
                nc.vector.tensor_tensor(v8(h[:, g]), b3(5), rows_bc(K["b2_rows"], 8), ALU.add).then_inc(S["h_set"], 1)
                dve.wait_ge(S["h_set"], g + 1)
                centre(v8(hc[:]), v8(h[:, g]), "x_centred")
                dve.wait_ge(S["x_sq"], g + 1)
                variance(sq)
                rsqrt(st_r[:, :], 8)
                nc.vector.tensor_tensor(v8(x[:, g]), v8(hc[:]), bc(st_r[:, :], D), ALU.mult).then_inc(S["x_set"], 1)
                if g == 0:
                    constants()
                yield

            def project(g):
                dve.wait_ge(S["xt_set"], g + 1)
                if g:
                    dve.wait_ge(S["ksk_mm"], g)
                link(nc.vector.tensor_tensor_scan(cx[:, :], ones[:, :], x_t[:, :], 0.0, ALU.mult, ALU.add))
                nc.vector.tensor_tensor(cx[:, :], cx[:, :], invpos[:, :], ALU.mult).then_inc(S["cx_set"], 1)
                yield

                def joint(c, i):
                    dve.wait_ge(S["vk_mm"], NC * g + c + 1)
                    nc.vector.tensor_tensor(vk[:, g, c], bank[i][:, 0:VK], K["vk_b"], ALU.add).then_inc(S["vk_set"], 1)

                joint(0, 3)
                joint(1, 0)
                yield
                dve.wait_ge(S["z_mm"], g + 1)
                nc.vector.tensor_tensor(zg[:, g, 0:32].rearrange("p (t h) -> p t h", h=H),
                                        bank[1][:, 0:32].rearrange("p (t h) -> p t h", h=H), rows_bc(K["hop_b2w"], 8), ALU.add)
                nc.vector.tensor_scalar(zg[:, g, 32:40], bank[1][:, 32:40], K["sg_b2"], None, ALU.add).then_inc(S["zg_set"], 1)
                joint(2, 3)
                joint(3, 0)
                dve.wait_ge(S["tg_set"], g + 1)
                nc.vector.tensor_scalar(gate[:, g], tg[:, g, 32:40], 0.5, 0.5, ALU.mult, ALU.add).then_inc(S["gate_set"], 1)
                yield
                for k, i in ((0, 2), (1, 3)):
                    dve.wait_ge(S["center_mm"], 2 * g + k + 1)
                    nc.vector.tensor_tensor(t_c[:, g, 4 * k:4 * k + 4], bank[i][:, :].rearrange("p (t q) -> p t q", q=P),
                                            rows_bc(K["hop_b2c"], 4), ALU.add).then_inc(S["center_set"], 1)
                dve.wait_ge(S["st_mm"], g + 1)
                nc.vector.tensor_tensor(kph[:, g, 1], bank[1][:, 0:256].rearrange("p (t q) -> p t q", q=PH),
                                        rows_bc(K["ksk_b2"], 8), ALU.add).then_inc(S["st_set"], 1)
                dve.wait_ge(S["gate_mm"], g + 1)
                nc.vector.tensor_copy(gsum[:, g], bank[0][:, 0:8]).then_inc(S["gate_read"], 1)
                dve.wait_ge(S["vk_set"], NC * (g + 1))
                gate2 = gate[:, g].rearrange("p (c f) -> p c f", f=2).unsqueeze(3).broadcast_to([P, NC, NH_, D])
                link(nc.vector.tensor_tensor(values(g), values(g), gate2, ALU.mult))
                yield

            def queries(g):
                link(nc.vector.tensor_scalar(wden[:, :], tg[:, g, 0:32], 1.1, None, ALU.add))
                link(nc.vector.tensor_tensor(wden[:, :], wden[:, :], wden[:, :], ALU.mult))
                link(nc.vector.tensor_scalar(wden[:, :], wden[:, :], 1e-6, None, ALU.add))
                link(nc.vector.reciprocal(wden[:, :], wden[:, :]))
                nc.vector.tensor_tensor(wexp[:], wden[:, :].unsqueeze(2).broadcast_to([P, 32, W]),
                                        rows_bc(d_exp[:, :], 32), ALU.mult).then_inc(S["w_pre"], 1)
                dve.wait_ge(S["center_tanh"], 2 * g + 2)
                for c in range(NC):
                    part = lambda t: t[:, 2 * c:2 * c + 2].rearrange("p f (h q) -> p (f h) q", q=PH)
                    ins = nc.vector.scalar_tensor_tensor(out=part(th), in0=part(t_c[:, g]), scalar=0.5,
                                                         in1=rows_bc(turn[:, c], 2 * H), op0=ALU.mult, op1=ALU.add)
                link(ins)
                dve.wait_ge(S["kq_tanh"], g + 1)
                dve.wait_ge(S["st_tanh"], g + 1)
                if g:
                    dve.wait_ge(S["k_feat"], 2 * g)
                magnitude(kph_abs[:], kph[:, g]).then_inc(S["kph_abs_set"], 1)
                yield
                dve.wait_ge(S["w_exp"], g + 1)
                nc.vector.tensor_reduce(wden[:, :], wexp[:], AX_X, ALU.add)
                link(nc.vector.tensor_tensor(wtmp[:], wexp[:], rows_bc(ang_cos[:, NC * PH:], 32), ALU.mult))
                nc.vector.tensor_reduce(csum[:, 0], wtmp[:], AX_X, ALU.add)
                link(nc.vector.tensor_tensor(wexp[:], wexp[:], rows_bc(ang_sin[:, NC * PH:], 32), ALU.mult))
                link(nc.vector.tensor_reduce(csum[:, 1], wexp[:], AX_X, ALU.add))
                link(nc.vector.tensor_tensor(wscr[:, 0:2], csum[:], csum[:], ALU.mult))
                link(nc.vector.tensor_tensor(wscr[:, 0], wscr[:, 0], wscr[:, 1], ALU.add))
                nc.vector.tensor_scalar(rs_v[:, 0:32], wscr[:, 0], 1e-30, None, ALU.max)
                link(nc.vector.tensor_scalar(rs_v[:, 32:40], gsum[:, g], 1.0, float(PH), ALU.max, ALU.mult))
                rsqrt(rs_a[:, 0:40], 40)
                nc.vector.tensor_copy(gcr[:, :], rs_a[:, 32:40])
                link(nc.vector.tensor_tensor(wscr[:, 0], wscr[:, 0], rs_a[:, 0:32], ALU.mult))
                link(magnitude(wscr[:, 1], csum[:, 0]))
                link(nc.vector.scalar_tensor_tensor(out=wscr[:, 1], in0=wscr[:, 1], scalar=1e-30, in1=wscr[:, 0],
                                                    op0=ALU.add, op1=ALU.add))
                link(nc.vector.reciprocal(wscr[:, 1], wscr[:, 1]))
                nc.vector.tensor_tensor(wscr[:, 2], csum[:, 1], wscr[:, 1], ALU.mult).then_inc(S["at_arg"], 1)
                link(nc.vector.tensor_scalar(wden[:, :], wden[:, :], 1e-6, float(H * np.sqrt(PH)), ALU.add, ALU.mult))
                link(nc.vector.reciprocal(wden[:, :], wden[:, :]))
                nc.vector.tensor_tensor(mag[:, :], wscr[:, 0], wden[:, :], ALU.mult)
                dve.wait_ge(S["k_feat"], 2 * g + 1)
                stored_q = feat[:, g, 0, :, D:P]
                link(nc.vector.tensor_tensor(stored_q, stored_q, bc(gcr[:, :], D), ALU.mult))
                yield
                link(nc.vector.tensor_scalar(wscr[:, 4], csum[:, 0], 0.0, None, ALU.is_lt))
                dve.wait_ge(S["at_set"], g + 1)
                link(nc.vector.tensor_scalar(wscr[:, 1], wscr[:, 3], -2.0 / np.pi, 0.5, ALU.mult, ALU.add))
                link(nc.vector.tensor_tensor(wscr[:, 1], wscr[:, 1], wscr[:, 4], ALU.mult))
                link(nc.vector.scalar_tensor_tensor(out=phi[:, :], in0=wscr[:, 3], scalar=1.0 / np.pi,
                                                    in1=wscr[:, 1], op0=ALU.mult, op1=ALU.add))
                for k in range(2):
                    tiles = slice(4 * k, 4 * k + 4)
                    t3 = th[:, tiles].rearrange("p t (h q) -> p (t h) q", q=PH)
                    link(nc.vector.tensor_tensor(t3, t3, bc(phi[:, 16 * k:16 * k + 16], PH), ALU.add))
                    if g:
                        dve.wait_ge(S["cos_set"], 2 * g)
                    link(nc.vector.tensor_scalar(thn[:, tiles], th[:, tiles], ROUND, ROUND, ALU.add, ALU.subtract))
                    nc.vector.tensor_tensor(th[:, tiles], th[:, tiles], thn[:, tiles], ALU.subtract).then_inc(S["th_set"], 1)
                    dve.wait_ge(S["th_set"], 2 * g + k + 1)
                    magnitude(thn[:, tiles], th[:, tiles]).then_inc(S["tha_set"], 1)
                yield
                for k in range(2):
                    tiles = slice(4 * k, 4 * k + 4)
                    for n, done in ((1, "sin_set"), (0, "cos_set")):
                        dve.wait_ge(S[done], 2 * g + k + 1)
                        q3 = q_sc[:, n, tiles].rearrange("p t (h q) -> p (t h) q", q=PH)
                        link(nc.vector.tensor_tensor(q3, q3, bc(mag[:, 16 * k:16 * k + 16], PH), ALU.mult))
                    for n in range(2):
                        ins = nc.vector.tensor_tensor(q_sc[:, n, tiles, 0:2 * PH], q_sc[:, n, tiles, 0:2 * PH],
                                                      q_sc[:, n, tiles, 2 * PH:4 * PH], ALU.add)
                    link(ins)
                    for n in range(2):
                        ins = nc.vector.tensor_tensor(feat[:, g, 0, tiles, n * PH:(n + 1) * PH], q_sc[:, n, tiles, 0:PH],
                                                      q_sc[:, n, tiles, PH:2 * PH], ALU.add)
                    ins.then_inc(S["q_sum"], 1)
                yield

            def chunks(g):
                tri2 = K["tri"].unsqueeze(1).broadcast_to([P, 2, P])

                def masked(c):
                    at = g * NC + c
                    for k in range(2):
                        dve.wait_ge(S["s_mm"], 2 * at + k + 1)
                        if at >= 2:
                            dve.wait_ge(S["out_mm"], at - 1)
                        nc.vector.tensor_tensor(s_m[:, c % 2, k], bank[4 + k][:, 0:2 * P].rearrange("p (f l) -> p f l", f=2),
                                                tri2, ALU.mult).then_inc(S["s_masked"], 1)

                def chunk_state(c):
                    dve.wait_ge(S["state_mm"], 3 * g + c + 1)
                    if c == 0:
                        if g:
                            dve.wait_ge(S["out_mm"], NC * g)
                        nc.vector.tensor_copy(state[:, 0], bank[6][:, 0:P]).then_inc(S["state_set"], 1)
                    else:
                        dve.wait_ge(S["state_set"], 3 * g + c)
                        nc.vector.tensor_tensor(state[:, c], bank[6][:, 0:P], state[:, c - 1],
                                                ALU.add).then_inc(S["state_set"], 1)

                yield
                yield
                masked(0)
                yield
                for c in range(1, NC):
                    masked(c)
                    chunk_state(c - 1)
                    yield
                dve.wait_ge(S["out_mm"], NC * (g + 1))
                centre(v8(comb[:]), b3(7), "comb_centred")
                yield
                dve.wait_ge(S["comb_sq"], g + 1)
                variance(sq_c)
                rsqrt(st_r[:, :], 8)
                dve.wait_ge(S["attn_mm"], g + 1)
                link(nc.vector.tensor_tensor(v8(comb[:]), b3(5), bc(st_r[:, :], D), ALU.mult))
                dve.wait_ge(S["hx_set"], g + 1)
                nc.vector.tensor_tensor(v8(h3[:, g]), v8(comb[:]), v8(x[:, g]), ALU.add).then_inc(S["h3_set"], 1)
                yield

            def expert_weights():
                dve.wait_ge(ffn_in, 32)
                dve.wait_ge(S["w1_hi"], 2)
                hi = w1hi[:].bitcast(F32)
                nc.vector.tensor_tensor(w1lo[0:D, :], K["e_w1"][0:D, :], hi[0:D, :], ALU.subtract).then_inc(S["w1_lo"], 1)
                mr = slice(D, D + MASK_ROWS)
                link(nc.vector.tensor_tensor(mrow_lo[mr, :], mrow_in[mr, :], w1lo[mr, :].bitcast(F32), ALU.subtract))
                link(nc.vector.tensor_scalar(mrow_lo[mr, :], mrow_lo[mr, :], K["sel_lo"][mr, :], None, ALU.mult))
                nc.vector.scalar_tensor_tensor(out=w1lo[mr, :], in0=w1lo[mr, :].bitcast(F32), scalar=K["sel_hi"][mr, :],
                                               in1=mrow_lo[mr, :], op0=ALU.mult, op1=ALU.add).then_inc(S["w1_lo"], 1)

            def experts(g):
                dve.wait_ge(S["h3_set"], g + 1)
                centre(v8(x2[:]), v8(h3[:, g]), "x2_centred")
                if g == 0:
                    expert_weights()
                dve.wait_ge(S["x2_sq"], g + 1)
                variance(sq)
                rsqrt(st_r[:, :], 8)
                link(nc.vector.tensor_tensor(v8(x2[:]), v8(x2[:]), bc(st_r[:, :], D), ALU.mult))
                if g:
                    dve.wait_ge(S["xp2_mm"], 2 * g)
                link(nc.vector.tensor_copy(xhl[:, :, D:2 * D], v8(x2[:])))
                nc.vector.tensor_tensor(xhl[:, :, 0:D], v8(x2[:]), xhl[:, :, D:2 * D].bitcast(F32),
                                        ALU.subtract).then_inc(S["xhl_set"], 1)
                yield
                dve.wait_ge(S["score_mm"], g + 1)
                nc.vector.tensor_tensor(score[:], bank[3][:, 0:64].rearrange("p (t e) -> p t e", e=E),
                                        rows_bc(K["bg"], 8), ALU.add).then_inc(S["score_read"], 1)
                dve.wait_ge(S["score_read"], g + 1)
                chosen = [sel, sel2]
                for k in range(2):
                    link(nc.vector.tensor_reduce(best[:, :], score[:], AX_X, ALU.max))
                    link(nc.vector.tensor_tensor(chosen[k][:], score[:], bc(best[:, :], E), ALU.is_equal))
                    link(nc.vector.tensor_tensor(chosen[k][:], chosen[k][:], rows_bc(K["tie"], 8), ALU.mult))
                    link(nc.vector.tensor_reduce(best[:, :], chosen[k][:], AX_X, ALU.max))
                    link(nc.vector.tensor_tensor(chosen[k][:], rows_bc(K["tie"], 8), bc(best[:, :], E), ALU.is_equal))
                    if k == 0:
                        link(nc.vector.scalar_tensor_tensor(out=score[:], in0=sel[:], scalar=-3.0e38, in1=score[:],
                                                            op0=ALU.mult, op1=ALU.add))
                link(nc.vector.tensor_tensor(xhl[:, :, 2 * D + E:2 * D + 2 * E], sel[:], sel2[:], ALU.add))
                nc.vector.tensor_scalar(xhl[:, :, 2 * D:2 * D + E], xhl[:, :, 2 * D + E:2 * D + 2 * E].bitcast(F32), -1.0,
                                        1.0, ALU.mult, ALU.add).then_inc(S["mask_set"], 1)
                yield
                yield
                for n in range(16):
                    yield
                dve.wait_ge(S["yt_mm"], g + 1)
                yt = bank[0][:, :].rearrange("p (c k d) -> p k c d", k=2, d=D)
                for k in range(2):
                    ins = nc.vector.tensor_tensor(v8(h[:, g])[:, 4 * k:4 * k + 4], yt[:, k],
                                                  v8(h3[:, g])[:, 4 * k:4 * k + 4], ALU.add)
                ins.then_inc(S["y_set"], 1)
                yield

            follow({"T": token, "P": project, "Q": queries, "C": chunks, "X": experts})


def kernel(x, mask_BSS_b0_1, fside_BSS_rel_dist, L0_tok_atom_embed, L0_tok_neighbor_embed, L0_tok_w_rd, L0_tok_w1,
           L0_tok_b1, L0_tok_gamma, L0_tok_beta, L0_tok_w2, L0_tok_b2, L0_attn_pos_phases, L0_attn_window_deltas,
           L0_attn_mc_w, L0_attn_mc_b, L0_attn_hop_w1, L0_attn_hop_b1, L0_attn_hop_w2, L0_attn_hop_b2, L0_attn_cpe_w,
           L0_attn_cpe_b, L0_attn_ve_w, L0_attn_ve_b, L0_attn_kce_w, L0_attn_kce_b, L0_attn_ksk_w1, L0_attn_ksk_b1,
           L0_attn_ksk_w2, L0_attn_ksk_b2, L0_attn_sg_w1, L0_attn_sg_b1, L0_attn_sg_w2, L0_attn_sg_b2, L0_attn_ln_g,
           L0_attn_ln_b, L0_attn_out_w, L0_attn_out_b, L0_ffn_Wg, L0_ffn_bg, L0_ffn_W1, L0_ffn_b1, L0_ffn_W2, L0_ffn_b2):
    import concourse.bacc as bacc
    from concourse.bass_utils import run_bass_kernel_spmd

    f = np.float32
    arr = lambda t: np.asarray(t)
    row = lambda t: np.tile(arr(t)[None, :], (P, 1))
    col = lambda t, n=1: np.tile(arr(t).reshape(-1), n)[:, None]

    def bd(w):
        w = arr(w)
        o = np.zeros((2 * w.shape[0], 2 * w.shape[1]), f)
        o[:w.shape[0], :w.shape[1]] = w
        o[w.shape[0]:, w.shape[1]:] = w
        return o

    def pack(table, parts):
        at, n = offsets(table)
        o = np.zeros((P, n), f)
        for name, (rows, a, b) in at.items():
            o[:rows, a:b] = parts[name]
        return o

    w1, ksk1, hop1 = arr(L0_tok_w1), arr(L0_attn_ksk_w1), arr(L0_attn_hop_w1)
    hop2 = arr(L0_attn_hop_w2).reshape(D, H, PH + 1)
    hopb2 = arr(L0_attn_hop_b2).reshape(H, PH + 1)
    pp = arr(L0_attn_pos_phases)[:L]
    twice = lambda w: np.concatenate([arr(w), arr(w)], axis=1)
    early = pack(EARLY, {
        "atom_T1": np.concatenate([arr(L0_tok_atom_embed).T, np.ones((1, ATOMS), f)]),
        "neigh_T": arr(L0_tok_neighbor_embed).T,
        "w1a_b1": np.concatenate([w1[:D], arr(L0_tok_b1)[None, :]]), "w1b": w1[D:], "w_rd": col(L0_tok_w_rd),
        "part_id": np.arange(P, dtype=f)[:, None], "gamma": col(L0_tok_gamma, 2), "beta": col(L0_tok_beta, 2),
        "w2_bd": bd(L0_tok_w2), "b2_rows": row(L0_tok_b2), "ident": np.eye(P, dtype=f),
        "tri": np.triu(np.ones((P, P), f))})
    late = pack(LATE, {
        "pp_T": pp.T, "pp_tok": pp.reshape(NC, P, PH).transpose(1, 0, 2).reshape(P, NC * PH),
        "deltas": row(L0_attn_window_deltas), "hop1x_bd": bd(hop1[:D]), "hop1p": twice(hop1[D:]),
        "hop_b1": col(L0_attn_hop_b1, 2), "ksk1x_bd": bd(ksk1[:D]), "kce_T_bd": bd(arr(L0_attn_kce_w).T),
        "ksk1c_bd": bd(ksk1[D:]), "ksk1c_dup": twice(ksk1[D:]), "kce_b": col(L0_attn_kce_b),
        "ksk_b1": col(L0_attn_ksk_b1, 2),
        "vk_bd": np.concatenate([bd(L0_attn_mc_w), bd(L0_attn_ve_w), bd(L0_attn_cpe_w)], axis=1),
        "vk_b": row(np.concatenate([arr(t) for t in (L0_attn_mc_b, L0_attn_mc_b, L0_attn_ve_b, L0_attn_ve_b,
                                                     L0_attn_cpe_b, L0_attn_cpe_b)])),
        "sg1_bd": bd(L0_attn_sg_w1), "sg_b1": col(L0_attn_sg_b1, 2), "sg2_bd": bd(L0_attn_sg_w2),
        "sg_b2": col(L0_attn_sg_b2, P), "ksk2_bd": bd(L0_attn_ksk_w2), "ksk_b2": row(L0_attn_ksk_b2),
        "hop2c_bd": bd(hop2[:, :, :PH].reshape(D, P)), "hop_b2c": row(hopb2[:, :PH].reshape(P)),
        "hop2w_bd": bd(hop2[:, :, PH]), "hop_b2w": row(hopb2[:, PH]),
        "ln_g": col(L0_attn_ln_g, 2), "out_bd": bd(L0_attn_out_w), "ln_b": np.tile(col(L0_attn_ln_b), (1, P)),
        "out_w": arr(L0_attn_out_w), "out_b": row(L0_attn_out_b)})
    e_w1 = arr(L0_ffn_W1).transpose(1, 0, 2).reshape(D, E * HID)
    e_b2 = np.zeros((P, D), f)
    e_b2[D + E:D + 2 * E] = arr(L0_ffn_b2)
    which = np.arange(P)[:, None]
    ffn = pack(FFN, {
        "wg": np.tile(arr(L0_ffn_Wg), (2, 1)), "bg": row(L0_ffn_bg), "e_w1": np.tile(e_w1, (2, 1)),
        "e_w2": arr(L0_ffn_W2).transpose(1, 0, 2).reshape(HID, E * D), "e_b2": e_b2,
        "tie": np.tile(np.arange(E, 0, -1, dtype=f)[None, :], (P, 1)),
        "sel_hi": (which != D + 2 * E + 1).astype(f), "sel_lo": (which == D + 2 * E + 1).astype(f)})
    mrows = np.zeros((MASK_ROWS, E, HID), f)
    mrows[np.arange(E), np.arange(E)] = -BIG
    mrows[2 * E:2 * E + 2] = arr(L0_ffn_b1)
    dist_t = np.ascontiguousarray(arr(fside_BSS_rel_dist).transpose(0, 2, 1))
    mask_t = np.ascontiguousarray(arr(mask_BSS_b0_1).transpose(0, 2, 1)).view(np.int32)
    arrays = {"ids": arr(x).reshape(1, B * L), "dist": dist_t, "mask": mask_t,
              "early": early, "late": late, "ffn": ffn, "mrows": mrows.reshape(MASK_ROWS, E * HID)}
    nc = bacc.Bacc("TRN2", target_bir_lowering=False, num_devices=1)
    args = [nc.dram_tensor(f"in_{k}", a.shape, mybir.dt.from_np(a.dtype), kind="ExternalInput").ap()
            for k, a in arrays.items()]
    out = nc.dram_tensor("out", (B, L, D), F32, kind="ExternalOutput").ap()
    tower(nc, *args, out)
    r = run_bass_kernel_spmd(nc, [{f"in_{k}": a for k, a in arrays.items()}], core_ids=[0])
    return r.results[0]["out"]
```
